# Optimizing a Trainium2 kernel written in Bass

```python
import numpy as np
import jax
import jax.numpy as jnp

def _softmax(x, axis=-1):
    return jax.nn.softmax(x, axis=axis)

def _gelu(x):
    return jax.nn.gelu(x, approximate=True)

def _silu(x):
    return jax.nn.silu(x)

def _sigmoid(x):
    return jax.nn.sigmoid(x)

def _layernorm(x, axis=-1, eps=1e-05):
    m = jnp.mean(x, axis=axis, keepdims=True)
    v = jnp.var(x, axis=axis, keepdims=True)
    return (x - m) / jnp.sqrt(v + eps)

def _scatter_add(tgt, idx, src, axis=0):
    return tgt.at[idx].add(src)

def _segment_sum(src, seg, n):
    return jax.ops.segment_sum(src, seg, n)
kernel_name = 'mk_gnn_ffn_d1_gnn_r16_ef364f'

def setup_inputs(seed: int=0):
    np.random.seed(seed)
    _w = jnp.asarray

    def _rec_inputs():
        import jax
        import jax.numpy as jnp
        _gk = jax.random.key(seed)
        x = -6.415e-05 + 1 * jax.random.normal(jax.random.fold_in(_gk, 1), (625, 512), jnp.float32)
        src = jax.random.randint(jax.random.fold_in(_gk, 2), (20000,), 0, 625, jnp.int32)
        dst = jnp.minimum((625 * jax.random.uniform(jax.random.fold_in(_gk, 3), (20000,)) ** 2.0).astype(jnp.int32), 9999)
        _o = jnp.argsort(dst, stable=True)
        src = src[_o]
        dst = dst[_o]
        edge_attr_64 = 0.000279952 + 1.00013 * jax.random.normal(jax.random.fold_in(_gk, 11), (20000, 64), jnp.float32)
        return (x, src, dst, edge_attr_64)
    x, src, dst, edge_attr_64 = _rec_inputs()

    def _L0_gnn_setup():
        import jax, jax.numpy as jnp
        import numpy as np
        N_NODES = 1250
        N_EDGES = 20000
        HIDDEN = 512
        EDGE_DIM = 64
        LN_EPS = 1e-05

        def mish(x):
            return x * jnp.tanh(jax.nn.softplus(x))
        key = jax.random.key(seed)
        ks = jax.random.split(key, 8)
        s = lambda fan_in: 1.0 / np.sqrt(fan_in)
        return {'x': jax.random.normal(ks[0], (N_NODES, HIDDEN), dtype=jnp.float32), 'edge_index': jax.random.randint(ks[1], (2, N_EDGES), 0, N_NODES, dtype=jnp.int64), 'edge_attr': jax.random.normal(ks[2], (N_EDGES, EDGE_DIM), dtype=jnp.float32), 'W1': jax.random.normal(ks[3], (2 * HIDDEN + EDGE_DIM, HIDDEN), dtype=jnp.float32) * s(2 * HIDDEN + EDGE_DIM), 'b1': jnp.zeros((HIDDEN,), dtype=jnp.float32), 'W2': jax.random.normal(ks[4], (HIDDEN, HIDDEN), dtype=jnp.float32) * s(HIDDEN), 'b2': jnp.zeros((HIDDEN,), dtype=jnp.float32), 'W3': jax.random.normal(ks[5], (2 * HIDDEN, HIDDEN), dtype=jnp.float32) * s(2 * HIDDEN), 'b3': jnp.zeros((HIDDEN,), dtype=jnp.float32), 'W4': jax.random.normal(ks[6], (HIDDEN, HIDDEN), dtype=jnp.float32) * s(HIDDEN), 'b4': jnp.zeros((HIDDEN,), dtype=jnp.float32), 'gamma': jnp.ones((HIDDEN,), dtype=jnp.float32), 'beta': jnp.zeros((HIDDEN,), dtype=jnp.float32)}
    _L0_gnn_all = _L0_gnn_setup()
    _L0_gnn_in = {k: v for k, v in _L0_gnn_all.items() if k in ('W1', 'b1', 'W2', 'b2', 'W3', 'b3', 'W4', 'b4', 'gamma', 'beta')}
    del _L0_gnn_all

    def _L0_ffn_setup():
        import jax, jax.numpy as jnp
        import numpy as np
        B, T, I, H, S = (64, 128, 512, 512, 4)

        def _lstm_activate(gates, c):
            i, f, g, o = jnp.split(gates, 4, axis=-1)
            c_new = jax.nn.sigmoid(f) * c + jax.nn.sigmoid(i) * jnp.tanh(g)
            h_new = jax.nn.sigmoid(o) * jnp.tanh(c_new)
            return (h_new, c_new)
        key = jax.random.key(seed)
        ks = jax.random.split(key, 7)
        sc_i = 1.0 / np.sqrt(I)
        sc_h = 1.0 / np.sqrt(H)
        x = jax.random.normal(ks[0], (B, T, I), jnp.float32)
        W_ih = jax.random.normal(ks[1], (S, 4 * H, I), jnp.float32) * sc_i
        W_hh = jax.random.normal(ks[2], (S, 4 * H, H), jnp.float32) * sc_h
        b_ih = jax.random.normal(ks[3], (S, 4 * H), jnp.float32) * sc_h
        b_hh = jax.random.normal(ks[4], (S, 4 * H), jnp.float32) * sc_h
        W_sel = jax.random.normal(ks[5], (S, 2 * H + I), jnp.float32) * sc_h
        b_sel = jax.random.normal(ks[6], (S,), jnp.float32) * sc_h
        return {'x': x, 'W_ih': W_ih, 'W_hh': W_hh, 'b_ih': b_ih, 'b_hh': b_hh, 'W_sel': W_sel, 'b_sel': b_sel}
    _L0_ffn_all = _L0_ffn_setup()
    _L0_ffn_in = {k: v for k, v in _L0_ffn_all.items() if k in ('W_ih', 'W_hh', 'b_ih', 'b_hh', 'W_sel', 'b_sel')}
    del _L0_ffn_all
    return {'x': x, 'src': src, 'dst': dst, 'edge_attr_64': edge_attr_64, 'L0_gnn_W1': _L0_gnn_in['W1'], 'L0_gnn_b1': _L0_gnn_in['b1'], 'L0_gnn_W2': _L0_gnn_in['W2'], 'L0_gnn_b2': _L0_gnn_in['b2'], 'L0_gnn_W3': _L0_gnn_in['W3'], 'L0_gnn_b3': _L0_gnn_in['b3'], 'L0_gnn_W4': _L0_gnn_in['W4'], 'L0_gnn_b4': _L0_gnn_in['b4'], 'L0_gnn_gamma': _L0_gnn_in['gamma'], 'L0_gnn_beta': _L0_gnn_in['beta'], 'L0_ffn_W_ih': _L0_ffn_in['W_ih'], 'L0_ffn_W_hh': _L0_ffn_in['W_hh'], 'L0_ffn_b_ih': _L0_ffn_in['b_ih'], 'L0_ffn_b_hh': _L0_ffn_in['b_hh'], 'L0_ffn_W_sel': _L0_ffn_in['W_sel'], 'L0_ffn_b_sel': _L0_ffn_in['b_sel']}

def reference(x, src, dst, edge_attr_64, L0_gnn_W1, L0_gnn_b1, L0_gnn_W2, L0_gnn_b2, L0_gnn_W3, L0_gnn_b3, L0_gnn_W4, L0_gnn_b4, L0_gnn_gamma, L0_gnn_beta, L0_ffn_W_ih, L0_ffn_W_hh, L0_ffn_b_ih, L0_ffn_b_hh, L0_ffn_W_sel, L0_ffn_b_sel):
    import jax
    import jax.numpy as jnp

    def _L0_gnn_ref(x, edge_index, edge_attr, W1, b1, W2, b2, W3, b3, W4, b4, gamma, beta):
        import jax, jax.numpy as jnp
        import numpy as np
        N_NODES = 1250
        N_EDGES = 20000
        HIDDEN = 512
        EDGE_DIM = 64
        LN_EPS = 1e-05

        def mish(x):
            return x * jnp.tanh(jax.nn.softplus(x))
        src, dst = (edge_index[0], edge_index[1])
        edge_feat = jnp.concatenate([x[src], x[dst], edge_attr], axis=-1)
        h = mish(edge_feat @ W1 + b1)
        messages = mish(h @ W2 + b2)
        agg = jax.ops.segment_sum(messages, dst, num_segments=x.shape[0])
        u = mish(jnp.concatenate([x, agg], axis=-1) @ W3 + b3)
        out = u @ W4 + b4
        y = x + out
        mu = jnp.mean(y, axis=-1, keepdims=True)
        var = jnp.mean(jnp.square(y - mu), axis=-1, keepdims=True)
        return (y - mu) * jax.lax.rsqrt(var + LN_EPS) * gamma + beta

    def _L0_ffn_ref(x, W_ih, W_hh, b_ih, b_hh, W_sel, b_sel):
        import jax, jax.numpy as jnp
        import numpy as np
        B, T, I, H, S = (64, 128, 512, 512, 4)

        def _lstm_activate(gates, c):
            i, f, g, o = jnp.split(gates, 4, axis=-1)
            c_new = jax.nn.sigmoid(f) * c + jax.nn.sigmoid(i) * jnp.tanh(g)
            h_new = jax.nn.sigmoid(o) * jnp.tanh(c_new)
            return (h_new, c_new)
        Bx, Tx, Ix = x.shape
        Sx, fourH, _ = W_ih.shape
        Hx = fourH // 4
        c0 = jnp.zeros((Bx, Hx), x.dtype)
        g0 = x[:, 0] @ W_ih[0].T + b_ih[0] + b_hh[0]
        h, c = _lstm_activate(g0, c0)

        def step(carry, x_t):
            h, c = carry
            sel_in = jnp.concatenate([h, c, x_t], axis=-1)
            logits = sel_in @ W_sel.T + b_sel
            onehot = jax.nn.one_hot(jnp.argmax(logits, axis=-1), Sx, dtype=x_t.dtype)
            g_all = jnp.einsum('bi,sgi->bsg', x_t, W_ih) + jnp.einsum('bh,sgh->bsg', h, W_hh) + b_ih + b_hh
            g = jnp.einsum('bsg,bs->bg', g_all, onehot)
            h2, c2 = _lstm_activate(g, c)
            return ((h2, c2), h2)
        xs = jnp.swapaxes(x[:, 1:], 0, 1)
        (_, _), hs = jax.lax.scan(step, (h, c), xs)
        outputs = jnp.concatenate([h[:, None], jnp.swapaxes(hs, 0, 1)], axis=1)
        return outputs
    edge_index = jnp.stack([src, dst])
    x = x + _L0_gnn_ref(_layernorm(x, axis=-1), edge_index, edge_attr_64, L0_gnn_W1, L0_gnn_b1, L0_gnn_W2, L0_gnn_b2, L0_gnn_W3, L0_gnn_b3, L0_gnn_W4, L0_gnn_b4, L0_gnn_gamma, L0_gnn_beta)
    x = x + _L0_ffn_ref(_layernorm(x, axis=-1)[None], L0_ffn_W_ih, L0_ffn_W_hh, L0_ffn_b_ih, L0_ffn_b_hh, L0_ffn_W_sel, L0_ffn_b_sel)[0]
    return x

_drawn_inputs = setup_inputs


def setup_inputs(seed=0):
    import zlib

    import numpy as np

    out = dict(_drawn_inputs(seed))
    spreads = {'L0_gnn_b1': (0.0, 0.1),
     'L0_gnn_b2': (0.0, 0.1),
     'L0_gnn_b3': (0.0, 0.313),
     'L0_gnn_b4': (0.0, 0.372),
     'L0_gnn_gamma': (1.0, 0.2),
     'L0_gnn_beta': (0.0, 0.1)}
    factors = {}
    for name, (base, spread) in spreads.items():
        noise = np.random.default_rng([zlib.crc32(name.encode()), seed]).standard_normal(out[name].shape)
        drawn = base * np.exp(spread * noise) if base else spread * noise
        out[name] = jnp.asarray(drawn.astype(out[name].dtype))
    for name, factor in factors.items():
        out[name] = (out[name] * factor).astype(out[name].dtype)
    return out
```

```python
import concourse.bass as bass
from concourse import mybir
from contextlib import ExitStack

F32 = mybir.dt.float32
F16 = mybir.dt.float16
BF16 = mybir.dt.bfloat16
I32 = mybir.dt.int32
U32 = mybir.dt.uint32
ALU = mybir.AluOpType
ACT = mybir.ActivationFunctionType
AX = mybir.AxisListType

LANES = 128
LN_EPS = 1e-5
PI = 3.141592653589793


class Named:
    pass


class Sem:

    def __init__(self, ctx, nc, name):
        self.handle = ctx.enter_context(nc.semaphore(name))
        self.value = 0

    def after(self, instruction, by=1):
        instruction.then_inc(self.handle, by)
        self.value += by
        return self, self.value

    def mark(self):
        return self, self.value


def need(engine, *marks):
    for mark in marks:
        if mark is not None:
            engine.wait_ge(mark[0].handle, mark[1])


def spans(total, step=LANES):
    return [(at, min(step, total - at)) for at in range(0, total, step)]


class Mish:

    def __init__(self, nc, k, sems, x, kept, factor):
        n = x.shape[0]
        self.nc, self.x, self.kept, self.factor = nc, x, kept, factor
        self.half, self.right_angle = k.half[:n, :], k.right_angle[:n, :]
        self.copied, self.angle, self.sine, self.done = sems

    def keep(self, *needed):
        need(self.nc.vector, *needed)
        self.has_x = self.copied.after(self.nc.vector.tensor_copy(self.kept, self.x))
        return self.has_x

    def angles(self, *needed):
        s = self.nc.scalar
        need(s, self.has_x, *needed)
        step = self.angle.after(s.activation(self.factor, self.kept, ACT.Tanh, scale=0.5))
        need(s, step)
        self.has_angle = self.angle.after(s.activation(self.factor, self.factor, ACT.Arctan,
                                                       bias=self.half, scale=-0.5))

    def cosine(self):
        s = self.nc.scalar
        need(s, self.has_angle)
        self.has_factor = self.sine.after(s.activation(self.factor, self.factor, ACT.Sin,
                                                       bias=self.right_angle, scale=-2.0))

    def result(self, out=None, *needed):
        v = self.nc.vector
        need(v, self.has_factor, *needed)
        self.has_result = self.done.after(
            v.tensor_tensor(self.kept if out is None else out, self.kept, self.factor, ALU.mult))
        return self.has_result


def layer_norm(nc, sem, root_sem, x, out, stats, moments, eps, *needed):
    v = nc.vector
    need(v, *needed)
    step = sem.after(v.bn_stats(stats, x))
    need(v, step)
    step = sem.after(v.bn_aggr(moments, stats))
    need(v, step)
    need(nc.scalar, step)
    step = root_sem.after(nc.scalar.activation(moments[:, 1:2], moments[:, 1:2], ACT.Sqrt, bias=eps))
    need(v, step)
    step = sem.after(v.reciprocal(moments[:, 1:2], moments[:, 1:2]))
    need(v, step)
    return sem.after(v.tensor_scalar(out, x, moments[:, 0:1], moments[:, 1:2], ALU.subtract, ALU.mult))


def graph_layer(nc, outer, d, k):
    N, H = d.x.shape
    E = d.src_t.shape[0] * d.src_t.shape[1]
    ED = d.W1c.shape[0]
    KH = H // LANES
    nodes = spans(N)
    NT = len(nodes)
    edges = spans(d.n_edges)
    ET = len(edges)
    pe, act, dve, pool, sp = nc.tensor, nc.scalar, nc.vector, nc.gpsimd, nc.sync

    with ExitStack() as ctx:
        def sb(name, shape, dt=F32):
            return ctx.enter_context(nc.sbuf_tensor(name, shape, dt))

        def sem(name):
            return Sem(ctx, nc, name)

        W1 = sb("W1", [LANES, 2 * KH, H])
        W1c = sb("W1c", [ED, H])
        W2 = sb("W2", [LANES, KH, H])
        W3 = W1
        W4 = sb("W4", [LANES, KH, H])
        b1, b3, b4 = sb("b1", [LANES, H]), sb("b3", [LANES, H]), sb("b4", [LANES, H])
        gamma, beta = sb("gamma", [LANES, H]), sb("beta", [LANES, H])
        b2_part = sb("b2_part", [1, 3, H], BF16)
        b2_rows = sb("b2_rows", [3, H], BF16)
        ones3 = sb("ones3", [3, LANES], BF16)
        zeros = sb("zeros", [LANES, H])
        xn = sb("xn", [LANES, NT, H])
        xnT = sb("xnT", [LANES, KH, N])
        stats, moments = sb("stats", [LANES, 6]), sb("moments", [LANES, 2])
        src_ix, dst_ix = sb("src_ix", [LANES, ET], I32), sb("dst_ix", [LANES, ET], I32)
        dst_f = sb("dst_f", [LANES, ET])
        node_no = sb("node_no", [LANES, N])
        proj = [sb(f"proj{n}", [LANES, H]) for n in range(5)]
        GB = 3
        from_src = [sb(f"from_src{n}", [LANES, H]) for n in range(GB)]
        from_dst = [sb(f"from_dst{n}", [LANES, H]) for n in range(GB)]
        EA_TILES = 8
        eaT = [sb(f"eaT{n}", [ED, EA_TILES * LANES]) for n in range(2)]
        onehot = [sb(f"onehot{n}", [LANES, N]) for n in range(2)]
        ROUND, LIVES = 4, 3
        hT = [sb(f"hT{n}", [LANES, KH, LANES]) for n in range(LIVES * ROUND)]
        msg = [sb(f"msg{n}", [LANES, H]) for n in range(LIVES * ROUND)]
        h_factor = [sb(f"h_factor{n}", [LANES, KH, LANES]) for n in range(ROUND)]
        m_factor = [sb(f"m_factor{n}", [LANES, H]) for n in range(ROUND)]
        b2, b2_rest = proj[4][0:1, :], m_factor[0][0:1, :]
        PAIR = 2
        rows = ET_rows = d.dst_rows.shape[0]
        per_row = d.dst_rows.shape[1] // LANES
        dst_by_tile = sb("dst_by_tile", [rows, per_row * LANES], I32)
        dst_by_tile_f = sb("dst_by_tile_f", [rows, per_row, LANES])
        ends = sb("ends", [rows, per_row, 2])
        ends_chunk = sb("ends_chunk", [rows, per_row, 2])
        ends_i = sb("ends_i", [rows, per_row, 2], I32)
        reach = sb("reach", [1, rows * per_row * 2], I32)
        ps = k.ps
        agg = ps[:NT]
        h_pre = ps[NT]
        m_pre = ps[NT + 1:NT + 3]

        loaded = {n: sem(f"ld_{n}") for n in
                  ("W1", "W1c", "W2", "W3", "W4", "bias", "src", "dst", "dstr", "b2")}
        x_in = [sem(f"x_in{m}") for m in range(NT)]
        ones_done, dve_own = sem("ones_done"), sem("dve_own")

        def load(name, dst, src, engine=sp):
            return loaded[name].after(engine.dma_start(dst, src), 16)

        x_here = []
        for m, (at, n) in enumerate(nodes):
            x_here.append(x_in[m].after(sp.dma_start(k.x1[:n, m, :], d.x[at:at + n, :]), 16))
        W1_here = load("W1", W1[:, :, :], d.W1ab.rearrange("(k p) n -> p k n", p=LANES))
        for t, s in ((b1, d.b1), (b3, d.b3), (b4, d.b4), (gamma, d.gamma), (beta, d.beta)):
            bias_here = load("bias", t[:, :], s.rearrange("(a n) -> a n", a=1).broadcast_to([LANES, H]), act)
        b2_here = load("b2", b2[:, :], d.b2.rearrange("(a n) -> a n", a=1), act)
        dstr_here = load("dstr", dst_by_tile[:, :], d.dst_rows, act)
        src_here = load("src", src_ix[:, :], d.src_t, act)
        dst_here = load("dst", dst_ix[:, :], d.dst_t, act)
        W1c_here = load("W1c", W1c[:, :], d.W1c)
        W2_here = load("W2", W2[:, :, :], d.W2.rearrange("(k p) n -> p k n", p=LANES))

        consts = sem("gnn_consts")
        ones_here = consts.after(pool.memset(ones3[:, :], 1.0))
        consts.after(pool.memset(zeros[:, :], 0.0))
        consts_here = consts.after(pool.iota(node_no[:, :], [[1, N]], base=0, channel_multiplier=0,
                                             allow_small_or_imprecise_dtypes=True))

        root, ln, tr, xnT_ev = sem("root"), sem("ln"), sem("tr"), sem("xnT_ev")
        xn_here = []
        for m, (at, n) in enumerate(nodes):
            xn_here.append(layer_norm(nc, ln, root, k.x1[:n, m, :], xn[:n, m, :], stats[:n, :], moments[:n, :],
                                      k.eps[:n, :], x_here[m]))
        xnT_here = []
        for m, (at, n) in enumerate(nodes):
            bank = ps[m % 2]
            need(pe, xn_here[m], k.ident_here, xnT_here[m - 2] if m >= 2 else None)
            for c in range(KH):
                last = pe.transpose(bank[:, c * LANES:c * LANES + n], xn[:n, m, c * LANES:(c + 1) * LANES],
                                    k.ident[:n, :n])
            mark = tr.after(last)
            need(act, mark)
            view = bank[:, :].rearrange("p (c n) -> p c n", c=KH)[:, :, :n]
            xnT_here.append(xnT_ev.after(act.activation(xnT[:, :, at:at + n], view, ACT.Copy)))
        pj, pj_ev, pj_out = sem("pj"), sem("pj_ev"), [sem(f"pj_out{n}") for n in range(5)]
        evicted, stored = [None] * 4, [None] * 4
        need(pe, W1_here, *xnT_here[-2:])
        for m, (at, n) in enumerate(nodes):
            for half, dram in enumerate((d.P, d.Q)):
                slot = (2 * m + half) % 4
                bank = ps[2 + slot]
                need(pe, evicted[slot])
                for c in range(KH):
                    last = pe.matmul(bank[:n, :], xnT[:, c, at:at + n], W1[:, half * KH + c, :],
                                     start=(c == 0), stop=(c == KH - 1))
                pj_last = mark = pj.after(last)
                if half == 0:
                    need(act, mark, stored[slot])
                    evicted[slot] = pj_ev.after(act.activation(proj[slot][:n, :], bank[:n, :], ACT.Copy))
                else:
                    need(dve, mark, stored[slot], bias_here)
                    evicted[slot] = ones_done.after(dve.tensor_tensor(proj[slot][:n, :], bank[:n, :], b1[:n, :], ALU.add))
                need(sp, evicted[slot])
                stored[slot] = pj_out[slot].after(sp.dma_start(dram[at:at + n, :], proj[slot][:n, :]), 16)
        need(sp, pj_last)
        load("W3", W3[:, :, :], d.W3.rearrange("(k p) n -> p k n", p=LANES))
        load("W4", W4[:, :, :], d.W4.rearrange("(k p) n -> p k n", p=LANES))

        need(dve, b2_here, dst_here, dstr_here, consts_here)
        step = None
        rest = b2
        for part in range(3):
            step = dve_own.after(dve.tensor_copy(b2_part[:, part, :], rest[:, :]))
            need(dve, step)
            if part < 2:
                step = dve_own.after(dve.tensor_tensor(b2_rest[:, :], rest[:, :], b2_part[:, part, :], ALU.subtract))
                need(dve, step)
            rest = b2_rest
        need(sp, step)
        b2_sent = loaded["b2"].after(sp.dma_start(b2_rows[:, :], b2_part[:, :, :]), 16)

        step = dve_own.after(dve.tensor_copy(dst_f[:, :], dst_ix[:, :]))
        step = dve_own.after(dve.tensor_copy(dst_by_tile_f[:, :, :], dst_by_tile[:, :].rearrange("r (a n) -> r a n", n=LANES)))
        need(dve, step)
        dve_own.after(dve.tensor_reduce(ends[:, :, 0], dst_by_tile_f[:, :, :], AX.X, ALU.min))
        step = dve_own.after(dve.tensor_reduce(ends[:, :, 1], dst_by_tile_f[:, :, :], AX.X, ALU.max))
        need(dve, step)
        step = dve_own.after(dve.tensor_scalar(ends_chunk[:, :, :], ends[:, :, :], float(LANES), None, ALU.is_ge))
        for j in range(2, NT):
            need(dve, step)
            step = dve_own.after(dve.scalar_tensor_tensor(ends_chunk[:, :, :], ends[:, :, :], float(j * LANES),
                                                          ends_chunk[:, :, :], ALU.is_ge, ALU.add))
        need(dve, step)
        dst_ready = dve_own.after(dve.tensor_copy(ends_i[:, :, :], ends_chunk[:, :, :]))
        need(sp, dst_ready)
        mark = loaded["dstr"].after(sp.dma_start(d.reach, ends_i[:, :, :].rearrange("r a b -> r (a b)")), 16)
        need(sp, mark)
        reach_here = loaded["dstr"].after(sp.dma_start(reach[:, :], d.reach.rearrange("(o r) c -> o (r c)", o=1)), 16)

        gather_a = [sem(f"gather_a{n}") for n in range(GB)]
        gather_b = [sem(f"gather_b{n}") for n in range(GB)]
        ea_in = [sem(f"ea_in{n}") for n in range(2)]
        h_sem, m_sem, agg_sem = sem("h_sem"), sem("m_sem"), sem("agg_sem")
        h_mish = [sem(f"h_{n}") for n in ("copied", "angle", "sine", "done")]
        m_mish = [sem(f"m_{n}") for n in ("copied", "angle", "sine", "done")]
        hot_sem = sem("hot_sem")
        gathered, h_done, m_done, agg_done = {}, {}, {}, {}
        h_of, m_of, hot_done, ea_done = {}, {}, {}, {}

        need(pool, *[s for s in stored if s], src_here, dst_here)

        def gather(i):
            at, n = edges[i]
            slot = i % GB
            need(pool, h_done.get(i - GB))
            a = gather_a[slot].after(pool.indirect_dma_start(
                from_src[slot][:n, :], None, d.P, bass.IndirectOffsetOnAxis(ap=src_ix[:n, i:i + 1], axis=0)), 16)
            b = gather_b[slot].after(pool.indirect_dma_start(
                from_dst[slot][:n, :], None, d.Q, bass.IndirectOffsetOnAxis(ap=dst_ix[:n, i:i + 1], axis=0)), 16)
            gathered[i] = (a, b)

        def load_attr(g):
            if g * EA_TILES >= ET:
                return
            at = g * EA_TILES * LANES
            n = min(EA_TILES * LANES, d.n_edges - at)
            need(sp, h_done.get((g - 1) * EA_TILES - 1) if g >= 2 else None)
            ea_done[g] = ea_in[g % 2].after(sp.dma_start(eaT[g % 2][:, :n], d.eaT[:, at:at + n]), 16)

        unsignalled = []

        def signalled_by(mark):
            for i in unsignalled:
                agg_done[i] = mark
            unsignalled.clear()

        def first_product(i):
            at, n = edges[i]
            slot, g = i % GB, i // EA_TILES
            need(pe, *gathered[i], ea_done[g], h_of[i - 1].has_x if i else None)
            lo = (i % EA_TILES) * LANES
            for c in range(KH):
                cols = slice(c * LANES, (c + 1) * LANES)
                out = h_pre[:, c * LANES:c * LANES + n]
                pe.matmul(out, from_src[slot][:n, cols], k.ident[:n, :n], start=True, stop=False, is_transpose=True)
                pe.matmul(out, from_dst[slot][:n, cols], k.ident[:n, :n], start=False, stop=False, is_transpose=True)
                last = pe.matmul(out, W1c[:, cols], eaT[g % 2][:, lo:lo + n], start=False, stop=True)
            h_done[i] = h_sem.after(last)
            signalled_by(h_done[i])

        def second_product(i):
            at, n = edges[i]
            bank = m_pre[i % 2]
            need(pe, h_of[i].has_result, m_of[i - 2].has_x if i >= 2 else None)
            pe.matmul(bank[:n, :], ones3[:, :n], b2_rows[:, :], start=True, stop=False)
            for c in range(KH):
                last = pe.matmul(bank[:n, :], hT[i % len(hT)][:, c, :n], W2[:, c, :], start=False, stop=(c == KH - 1))
            m_done[i] = m_sem.after(last)
            signalled_by(m_done[i])

        lowest, highest = pe.alloc_register("lowest_chunk"), pe.alloc_register("highest_chunk")

        def aggregate(i):
            at, n = edges[i]
            need(pe, m_of[i].has_result, hot_done[i])
            pe.reg_load(lowest, reach[0:1, 2 * i:2 * i + 1])
            pe.reg_load(highest, reach[0:1, 2 * i + 1:2 * i + 2])
            for c, (first, width) in enumerate(nodes):
                with pe.If_cmp(lowest, c, "IS_LE"):
                    with pe.If_cmp(highest, c, "IS_GE"):
                        pe.matmul(agg[c][:width, :], onehot[i % 2][:n, first:first + width], msg[i % len(msg)][:n, :],
                                  start=False, stop=True, skip_group_check=True)
                pe.end_ifs()
            unsignalled.append(i)

        for i in range(min(GB, ET)):
            gather(i)
        load_attr(0)
        load_attr(1)
        need(pe, W1c_here, W2_here, b2_sent, consts_here, reach_here, evicted[0], evicted[1], evicted[2], evicted[3])
        for c, (first, width) in enumerate(nodes):
            pe.matmul(agg[c][:width, :], zeros[:, :width], zeros[:, :], start=True, stop=True)

        def keep_h(i):
            n = edges[i][1]
            x = h_pre[:, :].rearrange("p (c n) -> p c n", c=KH)[:, :, :n]
            h_of[i] = Mish(nc, k, h_mish, x, hT[i % len(hT)][:, :, :n], h_factor[i % ROUND][:, :, :n])
            h_of[i].keep(h_done[i], m_done.get(i - len(hT)))

        def keep_m(i):
            n = edges[i][1]
            m_of[i] = Mish(nc, k, m_mish, m_pre[i % 2][:n, :], msg[i % len(msg)][:n, :], m_factor[i % ROUND][:n, :])
            m_of[i].keep(m_done[i], agg_done.get(i - len(msg)))

        def mark_targets(i):
            n = edges[i][1]
            if i - 2 in unsignalled:
                signalled_by(agg_sem.after(pe.drain()))
            need(dve, agg_done.get(i - 2))
            hot_done[i] = hot_sem.after(dve.tensor_scalar(onehot[i % 2][:n, :], node_no[:n, :], dst_f[:n, i:i + 1],
                                                          None, ALU.is_equal))

        def tiles(r):
            return [i for i in range(r * ROUND, (r + 1) * ROUND) if 0 <= i < ET]

        w_in, w_got = [sem(f"w_in{n}") for n in range(2)], sem("w_got")
        w_here, w_done = {}, {}

        def load_weights(q):
            if q < k.w_max.shape[1]:
                need(act, w_done.get(q - 2))
                w_here[q] = w_in[q % 2].after(act.dma_start(
                    k.w_stage[q % 2][:, :], d.W_hh[:, q * k.W_STAGE:(q + 1) * k.W_STAGE]), 16)

        def largest_weight(q):
            need(dve, w_here[q])
            w_done[q] = w_got.after(dve.tensor_reduce(k.w_max[:, q:q + 1], k.w_stage[q % 2][:, :], AX.X, ALU.max,
                                                      apply_absolute_value=True))

        load_weights(0)
        load_weights(1)
        for r in range(-2, -(-ET // ROUND) + 2):
            if 2 <= r < 2 + k.w_max.shape[1]:
                largest_weight(r - 2)
                load_weights(r)
            hs, ms = tiles(r + 1), tiles(r - 1)
            if hs or ms:
                act.preload_act_table_set("sigmoid_and_others")
                for i in hs:
                    h_of[i].angles(h_of[i - ROUND].has_result if i >= ROUND else None)
                for i in ms:
                    m_of[i].angles(m_of[i - ROUND].has_result if i >= ROUND else None)
                for t in [h_of[i] for i in hs] + [m_of[i] for i in ms]:
                    t.cosine()
            for j in range(ROUND):
                a, b, c = (r + 2) * ROUND + j, r * ROUND + j, (r - 2) * ROUND + j
                if 0 <= c < ET:
                    mark_targets(c)
                if a < ET:
                    first_product(a)
                    keep_h(a)
                if 0 <= b < ET:
                    second_product(b)
                    keep_m(b)
                if 0 <= c < ET:
                    aggregate(c)
                if j == ROUND - 2:
                    for i in hs:
                        h_of[i].result()
                if j == ROUND - 1:
                    for i in ms:
                        m_of[i].result()
                if a + GB < ET:
                    gather(a + GB)
                if a < ET and a % EA_TILES == EA_TILES - 1:
                    load_attr(a // EA_TILES + 2)

        signalled_by(agg_sem.after(pe.drain()))

        ag_ev, agT, agT_ev, u_sem, u_x, uT, uT_ev, o_sem = (sem(n) for n in (
            "ag_ev", "agT", "agT_ev", "u_sem", "u_x", "uT", "uT_ev", "o_sem"))
        fin, x2T, x2T_ev = sem("fin"), sem("x2T"), sem("x2T_ev")
        u_mish = [sem(f"u_{n}") for n in ("copied", "angle", "sine", "done")]
        W3_here, W4_here = (loaded["W3"], 16), (loaded["W4"], 16)
        agg_s = [proj[m] for m in range(NT)]
        aT, uT_s, u_of, u_factor = hT[0:2], hT[2:4], msg[0:NT], [*m_factor, h_factor[0]]
        u_mi = {}
        marks = {}
        for m, (at, n) in enumerate(nodes):
            need(act, agg_done[ET - 1])
            marks["ag", m] = ag_ev.after(act.activation(agg_s[m][:n, :], agg[m][:n, :], ACT.Copy))
        last_readers = [m_of[ET - 1].has_result, h_of[ET - 1].has_result, m_done[ET - 1]]
        for m, (at, n) in enumerate(nodes):
            need(pe, marks["ag", m], marks.get(("agT_ev", m - 1)), *last_readers)
            for c in range(KH):
                last = pe.transpose(h_pre[:, c * LANES:c * LANES + n], agg_s[m][:n, c * LANES:(c + 1) * LANES],
                                    k.ident[:n, :n])
            marks["agT", m] = agT.after(last)
            if m + 4 < NT:
                pass
            need(act, marks["agT", m], marks.get(("u_pre", m - 2)), *last_readers)
            view = h_pre[:, :].rearrange("p (c n) -> p c n", c=KH)[:, :, :n]
            marks["agT_ev", m] = agT_ev.after(act.activation(aT[m % 2][:, :, :n], view, ACT.Copy))
            bank = m_pre[m % 2]
            need(pe, W3_here, marks["agT_ev", m], marks.get(("u_x", m - 2)))
            for c in range(2 * KH):
                lhsT = xnT[:, c, at:at + n] if c < KH else aT[m % 2][:, c - KH, :n]
                last = pe.matmul(bank[:n, :], lhsT, W3[:, c, :], start=(c == 0), stop=(c == 2 * KH - 1))
            marks["u_pre", m] = u_sem.after(last)
            need(dve, marks["u_pre", m])
            marks["u_x", m] = u_x.after(dve.tensor_tensor(u_of[m][:n, :], bank[:n, :], b3[:n, :], ALU.add))
            factor = u_factor[m][:n, :] if m < ROUND else u_factor[m][:n, :, :].rearrange("p c n -> p (c n)")
            u_mi[m] = Mish(nc, k, u_mish, u_of[m][:n, :], u_of[m][:n, :], factor)
            u_mi[m].has_x = marks["u_x", m]
        act.preload_act_table_set("sigmoid_and_others")
        for m in range(NT):
            u_mi[m].angles()
        for m in range(NT):
            u_mi[m].cosine()
            marks["u", m] = u_mi[m].result()
        for m, (at, n) in enumerate(nodes):
            u = u_of[m][:n, :]
            bank = agg[m]
            need(pe, marks["u", m], marks["ag", m])
            for c in range(KH):
                last = pe.transpose(bank[:, c * LANES:c * LANES + n], u[:, c * LANES:(c + 1) * LANES], k.ident[:n, :n])
            marks["uT", m] = uT.after(last)
            need(act, marks["uT", m], marks.get(("o", m - 2)))
            view = bank[:, :].rearrange("p (c n) -> p c n", c=KH)[:, :, :n]
            marks["uT_ev", m] = uT_ev.after(act.activation(uT_s[m % 2][:, :, :n], view, ACT.Copy))
            need(pe, W4_here, marks["uT_ev", m])
            for c in range(KH):
                last = pe.matmul(bank[:n, :], uT_s[m % 2][:, c, :n], W4[:, c, :], start=(c == 0), stop=(c == KH - 1))
            marks["o", m] = o_sem.after(last)
            y = xn[:n, m, :]
            need(dve, marks["o", m])
            step = fin.after(dve.tensor_tensor(y, bank[:n, :], y, ALU.add))
            need(dve, step)
            step = fin.after(dve.tensor_tensor(y, y, b4[:n, :], ALU.add))
            step = layer_norm(nc, fin, root, y, y, stats[:n, :], moments[:n, :], k.eps[:n, :], step)
            need(dve, step)
            step = fin.after(dve.tensor_tensor(y, y, gamma[:n, :], ALU.mult))
            need(dve, step)
            step = fin.after(dve.tensor_tensor(y, y, beta[:n, :], ALU.add))
            need(dve, step)
            step = fin.after(dve.tensor_tensor(k.x1[:n, m, :], k.x1[:n, m, :], y, ALU.add))
            marks["x1", m] = step
            step = layer_norm(nc, fin, root, k.x1[:n, m, :], y, stats[:n, :], moments[:n, :], k.eps[:n, :], step)
            marks["xn2", m] = step
        for m, (at, n) in enumerate(nodes):
            bank = h_pre if m % 2 else m_pre[0]
            need(pe, marks["xn2", m], marks.get(("x2T_ev", m - 2)), marks["u_x", NT - 1], marks["agT_ev", NT - 1])
            for c in range(KH):
                last = pe.transpose(bank[:, c * LANES:c * LANES + n], xn[:n, m, c * LANES:(c + 1) * LANES],
                                    k.ident[:n, :n])
            mark = x2T.after(last)
            need(act, mark)
            view = bank[:, :].rearrange("p (c n) -> p c n", c=KH)[:, :, :n]
            marks["x2T_ev", m] = x2T_ev.after(act.activation(k.xn2T[:, :, at:at + n], view, ACT.Copy))
        k.x1_here = marks["x1", NT - 1]
        k.xn2T_here = marks["x2T_ev", NT - 1]
        nc.all_engine_barrier()


GATES = 4
G_IN, G_FORGET, G_INPUT, G_OUT = range(GATES)
H_SCALE = 4096.0
TOP_EXPONENT = 14
PARTS = 3


def power_of_two_scale(nc, k, sem, pe_sem, *needed):
    v, bank = nc.vector, k.ps[7]
    need(v, *needed)
    step = sem.after(v.tensor_reduce(k.w_top[:, 0:1], k.w_max[:, :], AX.X, ALU.max))
    need(nc.tensor, step)
    step = pe_sem.after(nc.tensor.transpose(bank[0:1, 0:LANES], k.w_top[:, 0:1], k.ident[:, :]))
    need(v, step)
    step = sem.after(v.tensor_reduce(k.w_top_row[:, :], bank[0:1, 0:LANES], AX.X, ALU.max))
    need(nc.tensor, step)
    step = pe_sem.after(nc.tensor.matmul(bank[:, LANES:LANES + 1], k.one_row[:, :], k.w_top_row[:, :],
                                         start=True, stop=True))
    need(v, step)
    step = sem.after(v.tensor_copy(k.w_top[:, 0:1], bank[:, LANES:LANES + 1]))
    for write in (
        lambda: v.tensor_scalar(k.exponent[:, :], k.w_top[:, :].bitcast(I32), 23, None, ALU.logical_shift_right),
        lambda: v.tensor_scalar(k.exponent[:, :], k.exponent[:, :], -1, TOP_EXPONENT + 254, ALU.mult, ALU.add),
        lambda: v.tensor_scalar(k.exponent[:, :], k.exponent[:, :], 253, None, ALU.min),
        lambda: v.tensor_scalar(k.w_scale[:, :].bitcast(I32), k.exponent[:, :], 23, None, ALU.logical_shift_left),
        lambda: v.tensor_scalar(k.exponent[:, :], k.exponent[:, :], -1, 254, ALU.mult, ALU.add),
        lambda: v.tensor_scalar(k.w_unscale[:, :].bitcast(I32), k.exponent[:, :], 23, None, ALU.logical_shift_left),
        lambda: v.tensor_scalar(k.w_unscale[:, :], k.w_unscale[:, :], 1.0 / H_SCALE, None, ALU.mult),
    ):
        need(v, step)
        step = sem.after(write())
    return step


def input_products(nc, d, k):
    N, H, S = d.x.shape[0], d.x.shape[1], d.S
    KH = H // LANES
    nodes = spans(N)
    pe, act, dve, pool, sp = nc.tensor, nc.scalar, nc.vector, nc.gpsimd, nc.sync
    with ExitStack() as ctx:
        def sb(name, shape, dt=F32):
            return ctx.enter_context(nc.sbuf_tensor(name, shape, dt))

        def sem(name):
            return Sem(ctx, nc, name)

        WB, OB, PB = 3, 3, 6
        W_in = [sb(f"W_in{n}", [LANES, KH, H]) for n in range(WB)]
        bias_a = [sb(f"bias_a{n}", [LANES, H]) for n in range(2)]
        bias_b = [sb(f"bias_b{n}", [LANES, H]) for n in range(2)]
        parts = [sb(f"parts{n}", [LANES, PARTS, H], BF16) for n in range(OB)]
        sel_x, sel_bias = sb("sel_x", [LANES, KH, S]), sb("sel_bias", [LANES, S])
        logits_out = sb("logits_out", [LANES, len(nodes), S])
        w_stage = k.w_stage
        W_here = [sem(f"W_here{n}") for n in range(WB)]
        bias_here = [sem(f"bias_here{n}") for n in range(2)]
        out_here = [sem(f"xg_out{n}") for n in range(OB)]
        sel_here, xl_out = sem("sel_here"), sem("xl_out")
        stage_here = [sem(f"stage{n}") for n in range(2)]
        bias_sum, xg, hi, lo, xl, xl_ev = (sem(n) for n in ("bias_sum", "xg", "hi", "lo", "xl", "xl_ev"))
        xg_v, xg_a = sem("xg_v"), sem("xg_a")

        sel_here.after(sp.dma_start(sel_x[:, :, :], d.Wsel[:, 2 * KH:3 * KH, :]), 16)
        sel_ready = sel_here.after(sp.dma_start(sel_bias[:, :], d.bsel.rearrange("(a n) -> a n", a=1)
                                                .broadcast_to([LANES, S])), 16)
        weights, biases, summed, products, biased, stored = {}, {}, {}, {}, {}, {}
        first, rest, second, third = {}, {}, {}, {}
        jobs = S * GATES

        def load(j):
            if j >= jobs:
                return
            need(pool, products.get((j - WB, len(nodes) - 1)))
            weights[j] = W_here[j % WB].after(pool.dma_start(W_in[j % WB][:, :, :], d.W_ih[j]), 16)

        def load_bias(j):
            if j >= jobs:
                return
            need(pool, biased.get((j - 2, len(nodes) - 1)))
            for t, s in ((bias_a, d.b_ih), (bias_b, d.b_hh)):
                biases[j] = bias_here[j % 2].after(
                    pool.dma_start(t[j % 2][:, :], s[j:j + 1, :].broadcast_to([LANES, H])), 16)

        for j in range(WB):
            load(j)
        load_bias(0)
        load_bias(1)

        need(pe, sel_ready)
        for m, (at, n) in enumerate(nodes):
            for c in range(KH):
                last = pe.matmul(k.ps[6][:n, m * S:(m + 1) * S], k.xn2T[:, c, at:at + n], sel_x[:, c, :],
                                 start=(c == 0), stop=(c == KH - 1))
        mark = xl.after(last)
        need(dve, mark)
        for m, (at, n) in enumerate(nodes):
            mark = xl_ev.after(dve.tensor_tensor(logits_out[:n, m, :], k.ps[6][:n, m * S:(m + 1) * S],
                                                 sel_bias[:n, :], ALU.add))
            need(sp, mark)
            k.xl_stored = xl_out.after(sp.dma_start(d.XL[at:at + n, :], logits_out[:n, m, :]), 16)

        slices = spans(k.W_hi.shape[1], k.W_STAGE)
        split = {}
        staged = {}

        def stage(q):
            if q >= len(slices):
                return
            at, n = slices[q]
            need(pool, split.get(q - 2))
            staged[q] = stage_here[q % 2].after(pool.dma_start(w_stage[q % 2][:, :n], d.W_hh[:, at:at + n]), 16)

        def split_slice(q):
            at, n = slices[q]
            need(act, staged[q], k.scale_ready)
            high = hi.after(act.activation(k.W_hi[:, at:at + n], w_stage[q % 2][:, :n], ACT.Copy,
                                           scale=k.w_scale[:, :]))
            need(dve, high)
            split[q] = lo.after(dve.scalar_tensor_tensor(k.W_lo[:, at:at + n], w_stage[q % 2][:, :n],
                                                         k.w_scale[:, :], k.W_hi[:, at:at + n],
                                                         ALU.mult, ALU.subtract))
            stage(q + 2)

        order = [(j, m) for j in range(jobs) for m in range(len(nodes))]

        def add_bias(count):
            (j, m), slot = order[count], count % OB
            n, bank = nodes[m][1], k.ps[count % PB]
            need(dve, products[j, m], summed[j])
            biased[j, m] = xg_v.after(dve.tensor_tensor(bank[:n, :], bank[:n, :], bias_a[j % 2][:n, :], ALU.add))
            need(act, biased[j, m], stored.get(count - OB))
            first[count] = xg_a.after(act.copy(parts[slot][:n, 0, :], bank[:n, :]))

        def split_rest(count):
            (j, m), slot = order[count], count % OB
            n, bank = nodes[m][1], k.ps[count % PB]
            need(dve, first[count])
            rest[count] = xg_v.after(dve.tensor_tensor(bank[:n, :], bank[:n, :], parts[slot][:n, 0, :], ALU.subtract))
            need(act, rest[count])
            second[count] = xg_a.after(act.copy(parts[slot][:n, 1, :], bank[:n, :]))

        def store(count):
            (j, m), slot = order[count], count % OB
            (at, n), bank = nodes[m], k.ps[count % PB]
            need(dve, second[count])
            third[count] = xg_v.after(dve.tensor_tensor(parts[slot][:n, 2, :], bank[:n, :], parts[slot][:n, 1, :],
                                                        ALU.subtract))
            need(sp, third[count])
            whole = n // 16 * 16
            for lo_row, rows in ((0, whole), (whole, n - whole)):
                if rows:
                    stored[count] = out_here[slot].after(
                        sp.dma_start(d.XG[at + lo_row:at + lo_row + rows, :, j, :],
                                     parts[slot][lo_row:lo_row + rows, :, :]), 16)

        stage(0)
        stage(1)
        q = 0
        for count in range(len(order) + 2):
            if count < len(order):
                j, m = order[count]
                at, n = nodes[m]
                if m == 0:
                    need(dve, biases[j])
                    summed[j] = bias_sum.after(dve.tensor_tensor(bias_a[j % 2][:, :], bias_a[j % 2][:, :],
                                                                 bias_b[j % 2][:, :], ALU.add))
                need(pe, weights[j] if m == 0 else None, third.get(count - PB))
                for c in range(KH):
                    last = pe.matmul(k.ps[count % PB][:n, :], k.xn2T[:, c, at:at + n], W_in[j % WB][:, c, :],
                                     start=(c == 0), stop=(c == KH - 1))
                products[j, m] = xg.after(last)
                add_bias(count)
            if 0 <= count - 1 < len(order):
                split_rest(count - 1)
            if 0 <= count - 2 < len(order):
                store(count - 2)
            if count < len(order):
                if m % 2 == 1 and q < len(slices):
                    split_slice(q)
                    q += 1
                if m == len(nodes) - 1:
                    load(j + WB)
                    load_bias(j + 2)
        while q < len(slices):
            split_slice(q)
            q += 1
        need(sp, *[stored[len(order) - 1 - n] for n in range(OB)], k.xl_stored)
        nc.all_engine_barrier()


def recurrence(nc, d, k):
    N, H, S = d.x.shape[0], d.x.shape[1], d.S
    KH = H // LANES
    R = PARTS * S * GATES
    pe, act, dve, pool, sp = nc.tensor, nc.scalar, nc.vector, nc.gpsimd, nc.sync
    UNROLL, HALF = 4, 2
    COPIES = ((0, 1), (1, 1), (2, 2))
    assert sum(n for _, n in COPIES) == KH
    FILL = ((512, 512, 512, 512), (256,), (512,) * 5, (512,))
    ITERATIONS = (N - 1) // UNROLL
    assert 1 + ITERATIONS * UNROLL == N
    with ExitStack() as ctx:
        def sb(name, shape, dt=F32):
            return ctx.enter_context(nc.sbuf_tensor(name, shape, dt))

        def sem(name):
            return Sem(ctx, nc, name)

        cell = [sb(f"cell{n}", [LANES, 5 * KH]) for n in range(2)]
        products = sb("products", [LANES, 2 * KH])
        out_gate, tanh_c = sb("out_gate", [LANES, KH]), sb("tanh_c", [LANES, KH])
        cell_sel = sb("cell_sel", [LANES, KH])
        h = sb("h", [LANES, UNROLL, KH])
        h_pair = sb("h_pair", [LANES, KH, 2], F16)
        gate_rows = sb("gate_rows", [LANES, H])
        x_rows = [sb(f"x_rows{n}", [R, HALF, H], BF16) for n in range(2)]
        x_logits = [sb(f"x_logits{n}", [1, HALF * S]) for n in range(2)]
        x_rows0 = sb("x_rows_first", [R, H], BF16)
        sel_h, sel_c = sb("sel_h", [LANES, KH, S]), sb("sel_c", [LANES, KH, S])
        pick_gate, pick_row = sb("pick_gate", [LANES, GATES]), sb("pick_row", [R, S, GATES], BF16)
        top, which = sb("top", [1, 8]), sb("which", [1, 8], U32)
        history = sb("history", [LANES, N, KH])
        rows_p, gates_p, logits_p = k.ps[0], k.ps[1], k.ps[2]
        gates_by = gates_p[:, 0:GATES * KH].rearrange("p (g c) -> p g c", c=KH)
        XG_rows = d.XG.rearrange("t p r n -> t (p r) n")
        W_hi = k.W_hi[:, :].rearrange("p (s c n) -> p s c n", s=S, c=KH)
        W_lo = k.W_lo[:, :].rearrange("p (s c n) -> p s c n", s=S, c=KH)

        setup, setup_v, first_in = sem("rec_setup"), sem("rec_setup_v"), sem("rec_first")
        x_in = [sem(f"x_in{n}") for n in range(2)]

        def load_half(t, half):
            x_in[half].after(sp.dma_start(x_rows[half][:, :, :],
                                           XG_rows[bass.ds(t, HALF), :, :].rearrange("t r n -> r t n")), 16)
            x_in[half].after(sp.dma_start(x_logits[half][:, :], d.XL1[:, bass.ds(t * S, HALF * S)]), 16)

        first_in.after(sp.dma_start(x_rows0[:, :], XG_rows[0, :, :]), 16)
        first_in.after(sp.dma_start(sel_h[:, :, :], d.Wsel[:, 0:KH, :]), 16)
        first_here = first_in.after(sp.dma_start(sel_c[:, :, :], d.Wsel[:, KH:2 * KH, :]), 16)
        load_half(1, 0)
        load_half(1 + HALF, 1)

        step = setup.after(pool.memset(pick_gate[:, :], 0.0))
        need(pool, step)
        for part in range(2):
            step = setup.after(pool.affine_select(out=pick_gate[:, :], in_=pick_gate[:, :], compare_op=ALU.not_equal,
                                                  fill=1.0, base=-part, pattern=[[-32, GATES]], channel_multiplier=1))
            need(pool, step)
        need(dve, step, first_here, k.scale_ready)
        blocks = k.ident[:R, :R].rearrange("p (a r) -> p a r", a=PARTS)
        row_of = pick_row[:, :, :].rearrange("p s g -> p (s g)")
        need(dve, setup_v.after(dve.tensor_tensor(row_of, blocks[:, 0, :], blocks[:, 1, :], ALU.add)))
        need(dve, setup_v.after(dve.tensor_tensor(row_of, row_of, blocks[:, 2, :], ALU.add)))
        step = setup_v.after(dve.tensor_scalar(pick_gate[:, :], pick_gate[:, :], k.w_unscale[:, :], None, ALU.mult))
        need(dve, step)
        setup_v.after(dve.tensor_scalar(pick_gate[:, G_IN:G_IN + 1], pick_gate[:, G_IN:G_IN + 1], 2.0, None, ALU.mult))
        setup_v.after(dve.tensor_scalar(pick_row[:, :, G_IN:G_IN + 1], pick_row[:, :, G_IN:G_IN + 1], 2.0, None, ALU.mult))
        setup_v.after(dve.tensor_scalar(sel_h[:, :, :], sel_h[:, :, :], 1.0 / H_SCALE, None, ALU.mult))
        setup_v.after(dve.tensor_scalar(sel_c[:, :, :], sel_c[:, :, :], 0.5, None, ALU.mult))
        setup_v.after(dve.memset(rows_p[:, :], 0.0))
        setup_v.after(dve.memset(logits_p[0:1, 0:8], -3.0e38))
        setup_v.after(dve.memset(cell[0][:, :], 0.0))
        step = setup_v.after(dve.memset(cell[1][:, :], 0.0))
        for e in (pe, act, dve, pool):
            need(e, step)
        act.preload_act_table_set("sigmoid_and_others")

        def turn_sem(name, consumer):
            s = sem(name)
            s.consumer = consumer
            return s

        rows_ready, copied = turn_sem("rows_ready", act), turn_sem("copied", pe)
        gates_ready, gates_tanh = turn_sem("gates_ready", act), turn_sem("gates_tanh", dve)
        own, c_act, c_tanh = turn_sem("own", dve), turn_sem("c_act", act), turn_sem("c_tanh", dve)
        picked, logits_ready = turn_sem("picked", pe), turn_sem("logits_ready", dve)
        c_pe, h_ready, pair_ready = (turn_sem(n, pe) for n in ("c_pe", "h_ready", "pair_ready"))
        released = [sem(f"released{n}") for n in range(2)]

        def take_off(*semaphores):
            for s in semaphores:
                s.consumer.sem_inc(s.handle, -s.value)
                s.value = 0

        def keep_clock(widths):
            for columns in widths:
                pe.matmul(k.ps[7][0:2, 0:columns], k.W_hi[:, 0:2], k.W_hi[:, 0:columns], start=True, stop=True)

        def select(u, half, v, turn):
            out, h_before = logits_p[0:1, 0:S], h[:, u, :]
            if v == 0:
                need(pe, (x_in[half], 32))
            pe.matmul(out, k.one_row[0:1, 0:1], x_logits[half][0:1, v * S:(v + 1) * S], start=True, stop=False)
            need(pe, c_pe.mark())
            for c in range(KH):
                pe.matmul(out, cell_sel[:, c:c + 1], sel_c[:, c, :], start=False, stop=False)
            keep_clock(FILL[1])
            need(pe, h_ready.mark())
            for c in range(KH):
                last = pe.matmul(out, h_before[:, c:c + 1], sel_h[:, c, :], start=False, stop=(c == KH - 1))
            need(dve, logits_ready.after(last))
            keep_clock(FILL[2])
            step = own.after(dve.max(top[:, :], logits_p[0:1, 0:8]))
            need(dve, step)
            mark = picked.after(dve.max_index(which[:, :], top[:, :], logits_p[0:1, 0:8]))
            if u == UNROLL - 1:
                dve.tensor_copy(flat[:, bass.ds(turn * (UNROLL * KH), UNROLL * KH)],
                                h[:, :, :].rearrange("p t c -> p (t c)"))
                take_off(own, gates_tanh, c_tanh, logits_ready)
            return mark

        def x_part(rows, s, stop=False):
            for c in range(KH):
                last = pe.matmul(gates_by[:, :, c], rows[:, c * LANES:(c + 1) * LANES], pick_row[:, s, :],
                                 start=(c == 0), stop=stop, skip_group_check=True)
            return last

        expert = pe.alloc_register("expert")

        def gates(u, half, v, which_mark):
            need(pe, which_mark)
            pe.reg_load(expert, which[0:1, 0:1])
            need(pe, pair_ready.mark())

            def arm(s):
                for n, part in enumerate((W_hi, W_lo)):
                    for c in range(KH):
                        for g in range(GATES):
                            last = pe.matmul(rows_p[32 * g:32 * g + 2, :], h_pair[:, c, :],
                                             part[:, s, c, g * H:(g + 1) * H], start=(n == c == 0),
                                             stop=(n == 1 and c == KH - 1))
                last.then_inc(rows_ready.handle, 1)
                x_part(x_rows[half][:, v, :], s)

            with pe.If_lt(expert, 2):
                with pe.If_lt(expert, 1):
                    arm(0)
                with pe.Else():
                    arm(1)
            with pe.Else():
                with pe.If_lt(expert, 3):
                    arm(2)
                with pe.Else():
                    arm(3)
            pe.end_ifs()
            if u == UNROLL - 1:
                take_off(rows_ready, gates_ready, c_act, copied, c_pe, h_ready, picked, pair_ready)
                for n in range(2):
                    pe.sem_inc(x_in[n].handle, -32)
            rows_ready.value += 1
            need(act, rows_ready.mark())
            chunk_copied = {}
            for first, count in COPIES:
                at = slice(first * LANES, (first + count) * LANES)
                chunk_copied[first] = copied.after(act.activation(gate_rows[:, at], rows_p[:, at], ACT.Copy))
            keep_clock(FILL[3])
            for c in range(KH):
                need(pe, chunk_copied.get(c))
                last = pe.matmul(gates_by[:, :, c], gate_rows[:, c * LANES:(c + 1) * LANES], pick_gate[:, :],
                                 start=False, stop=(c == KH - 1), skip_group_check=True)
                if c == 0 and v == HALF - 1:
                    last.then_inc(released[half].handle, 1)
            mark = gates_ready.after(last)
            keep_clock(FILL[0])
            return mark

        def update(u, gates_mark):
            this, following, h_out = cell[u % 2], cell[(u + 1) % 2], h[:, (u + 1) % UNROLL, :]
            need(act, gates_mark)
            tanhs = gates_tanh.after(act.activation(this[:, KH:5 * KH], gates_p[:, 0:GATES * KH], ACT.Tanh, scale=0.5))
            need(dve, tanhs)
            step = own.after(dve.scalar_tensor_tensor(products[:, :], this[:, 2 * KH:4 * KH], 1.0, this[:, 0:2 * KH],
                                                      ALU.add, ALU.mult))
            need(dve, step)
            c_done = c_act.after(dve.scalar_tensor_tensor(following[:, 0:KH], products[:, 0:KH], 0.5,
                                                          products[:, KH:2 * KH], ALU.mult, ALU.add))
            out_done = own.after(dve.tensor_scalar(out_gate[:, :], this[:, 4 * KH:5 * KH], 1.0, H_SCALE / 2,
                                                   ALU.add, ALU.mult))
            c_pe.after(dve.scalar_tensor_tensor(cell_sel[:, :], products[:, 0:KH], 0.5, products[:, KH:2 * KH],
                                                ALU.mult, ALU.add))
            need(act, c_done)
            tc = c_tanh.after(act.activation(tanh_c[:, :], following[:, 0:KH], ACT.Tanh, scale=0.5))
            need(dve, out_done, tc)
            h_ready.after(dve.tensor_tensor(h_out, out_gate[:, :], tanh_c[:, :], ALU.mult))
            step = own.after(dve.tensor_tensor(h_pair[:, :, 0], out_gate[:, :], tanh_c[:, :], ALU.mult))
            need(dve, step)
            pair_ready.after(dve.tensor_tensor(h_pair[:, :, 1], h_out, h_pair[:, :, 0], ALU.subtract))
            return step

        need(pe, first_here)
        mark = gates_ready.after(x_part(x_rows0, 0, stop=True))
        update(UNROLL - 1, mark)
        pe.sem_inc(rows_ready.handle, 1)
        act.sem_inc(copied.handle, len(COPIES))
        rows_ready.value, copied.value = 1, len(COPIES)

        engines = bass.OrderedEngineSet([mybir.EngineType.PE, mybir.EngineType.Activation, mybir.EngineType.DVE])
        flat = history[:, :, :].rearrange("p t c -> p (t c)")
        with nc.Fori(0, ITERATIONS, engines=engines) as turn:
            for u in range(UNROLL):
                half, v = divmod(u, HALF)
                which_mark = select(u, half, v, turn)
                mark = gates(u, half, v, which_mark)
                update(u, mark)

        with sp.Fori(0, ITERATIONS - 1) as turn:
            for half in range(2):
                need(sp, (released[half], 1))
                sp.sem_inc(released[half].handle, -1)
                load_half(turn * UNROLL + (1 + UNROLL + half * HALF), half)

        hist, back, total, out = sem("hist"), sem("back"), sem("total"), [sem("out_even"), sem("out_odd")]
        need(dve, own.mark())
        hist_here = hist.after(dve.tensor_copy(history[:, N - 1, :], h[:, 0, :]))
        results = [sb(f"result{n}", [LANES, H]) for n in range(2)]
        stored, added = {}, {}
        for m, (at, n) in enumerate(spans(N)):
            bank = k.ps[3 + m % 2]
            need(pe, hist_here, added.get(m - 2))
            for c in range(KH):
                last = pe.transpose(bank[:n, c * LANES:(c + 1) * LANES], history[:, at:at + n, c], k.ident[:, :])
            need(dve, back.after(last), stored.get(m - 2))
            added[m] = total.after(dve.scalar_tensor_tensor(results[m % 2][:n, :], bank[:n, :], 1.0 / H_SCALE,
                                                            k.x1[:n, m, :], ALU.mult, ALU.add))
            need(sp, added[m])
            stored[m] = out[m % 2].after(sp.dma_start(d.out[at:at + n, :], results[m % 2][:n, :]), 16)
        need(sp, stored[m - 1], stored[m])


def program(nc, d):
    with ExitStack() as ctx:
        k = Named()
        H, N = d.x.shape[1], d.x.shape[0]
        KH, S = H // LANES, d.S
        NT = len(spans(N))

        def sb(name, shape, dt=F32):
            return ctx.enter_context(nc.sbuf_tensor(name, shape, dt))

        k.ident = sb("ident", [LANES, LANES])
        k.half, k.right_angle, k.eps = sb("half", [LANES, 1]), sb("right_angle", [LANES, 1]), sb("eps", [LANES, 1])
        k.one_row = sb("one_row", [1, LANES])
        k.x1 = sb("x1", [LANES, NT, H])
        k.xn2T = sb("xn2T", [LANES, KH, N])
        k.W_STAGE = 1024
        k.w_stage = [sb(f"w_stage{n}", [LANES, k.W_STAGE]) for n in range(2)]
        k.w_max = sb("w_max", [LANES, d.W_hh.shape[1] // k.W_STAGE])
        k.w_top, k.w_top_row = sb("w_top", [LANES, 1]), sb("w_top_row", [1, 1])
        k.exponent = sb("exponent", [LANES, 1], I32)
        k.w_scale, k.w_unscale = sb("w_scale", [LANES, 1]), sb("w_unscale", [LANES, 1])
        k.ps = [ctx.enter_context(nc.psum_tensor(f"bank{n}", [LANES, 512], F32)) for n in range(8)]
        ready = Sem(ctx, nc, "ident_ready")
        ready.after(nc.gpsimd.memset(k.ident[:, :], 0.0))
        ready.after(nc.gpsimd.memset(k.half[:, :], 0.5))
        ready.after(nc.gpsimd.memset(k.right_angle[:, :], PI / 2))
        ready.after(nc.gpsimd.memset(k.one_row[:, :], 1.0))
        need(nc.gpsimd, ready.after(nc.gpsimd.memset(k.eps[:, :], LN_EPS)))
        k.ident_here = ready.after(nc.gpsimd.affine_select(
            out=k.ident[:, :], in_=k.ident[:, :], compare_op=ALU.not_equal, fill=1.0, base=0,
            pattern=[[-1, LANES]], channel_multiplier=1))
        need(nc.scalar, k.ident_here)
        graph_layer(nc, ctx, d, k)
        k.W_hi, k.W_lo = (sb(n, [LANES, d.W_hh.shape[1]], F16) for n in ("W_hi", "W_lo"))
        scale_v, scale_pe = Sem(ctx, nc, "scale_v"), Sem(ctx, nc, "scale_pe")
        k.scale_ready = power_of_two_scale(nc, k, scale_v, scale_pe)
        input_products(nc, d, k)
        recurrence(nc, d, k)
def kernel(**inputs):
    import numpy as np
    import concourse.bacc as bacc
    from concourse.bass_utils import run_bass_kernel_spmd as run
    nc = bacc.Bacc("TRN2", target_bir_lowering=False, num_devices=1)
    arrays, d = {}, Named()

    def give(name, a):
        a = np.ascontiguousarray(a)
        arrays["in_" + name] = a
        return nc.dram_tensor("in_" + name, a.shape, mybir.dt.from_np(a.dtype), kind="ExternalInput").ap()

    def by_tile(a):
        tiles = -(-a.shape[0] // LANES)
        full = np.zeros((tiles * LANES,), a.dtype)
        full[:a.shape[0]] = a
        return full.reshape(tiles, LANES)

    H = inputs["x"].shape[1]
    N = inputs["x"].shape[0]
    n_edges = inputs["src"].shape[0]
    W1 = np.asarray(inputs["L0_gnn_W1"])
    d.x = give("x", inputs["x"])
    d.W1ab = give("W1ab", W1[:2 * H])
    d.W1c = give("W1c", W1[2 * H:])
    d.W2, d.W3, d.W4, d.b1, d.b2, d.b3, d.b4, d.gamma, d.beta = (
        give(n, inputs["L0_gnn_" + n]) for n in ("W2", "W3", "W4", "b1", "b2", "b3", "b4", "gamma", "beta"))
    src, dst = np.asarray(inputs["src"]), np.asarray(inputs["dst"])
    d.src_t = give("src_t", by_tile(src).T)
    d.dst_t = give("dst_t", by_tile(dst).T)
    tiles = -(-n_edges // (2 * LANES)) * 2
    rows = np.concatenate([dst, np.repeat(dst[-1:], tiles * LANES - n_edges)])
    d.dst_rows = give("dst_rows", rows.reshape(tiles // 2, 2 * LANES))
    order = [2, 1, 0, 3]
    S = inputs["L0_ffn_W_ih"].shape[0]
    KH = H // LANES
    W_hh = np.asarray(inputs["L0_ffn_W_hh"]).reshape(S, GATES, H, KH, LANES)[:, order]
    d.W_hh = give("W_hh", W_hh.transpose(4, 0, 3, 1, 2).reshape(LANES, -1))
    W_ih = np.asarray(inputs["L0_ffn_W_ih"]).reshape(S, GATES, H, KH, LANES)[:, order]
    d.W_ih = give("W_ih", W_ih.transpose(0, 1, 4, 3, 2).reshape(S * GATES, LANES, KH, H))
    d.b_ih, d.b_hh = (give(n, np.asarray(inputs["L0_ffn_" + n]).reshape(S, GATES, H)[:, order].reshape(S * GATES, H))
                      for n in ("b_ih", "b_hh"))
    d.Wsel = give("Wsel", np.asarray(inputs["L0_ffn_W_sel"]).T.reshape(3 * KH, LANES, S).transpose(1, 0, 2))
    d.bsel = give("bsel", inputs["L0_ffn_b_sel"])
    d.eaT = give("eaT", np.asarray(inputs["edge_attr_64"]).T)
    d.n_edges, d.S = n_edges, S
    d.P = nc.dram_tensor("scratch_P", (N, H), F32, kind="Internal").ap()
    d.Q = nc.dram_tensor("scratch_Q", (N, H), F32, kind="Internal").ap()
    d.reach = nc.dram_tensor("scratch_reach", (tiles // 2, 4), I32, kind="Internal").ap()
    d.XG = nc.dram_tensor("scratch_XG", (N, PARTS, S * GATES, H), BF16, kind="Internal").ap()
    d.XL = nc.dram_tensor("scratch_XL", (N, S), F32, kind="Internal").ap()
    d.XL1 = d.XL.rearrange("(o t) s -> o (t s)", o=1)
    d.out = nc.dram_tensor("out_0", (N, H), F32, kind="ExternalOutput").ap()
    program(nc, d)
    r = run(nc, [arrays], core_ids=[0])
    return r.results[0]["out_0"]
```

```python
import concourse.bass as bass
from concourse import mybir
from contextlib import ExitStack

F32 = mybir.dt.float32
F16 = mybir.dt.float16
BF16 = mybir.dt.bfloat16
I32 = mybir.dt.int32
U32 = mybir.dt.uint32
ALU = mybir.AluOpType
ACT = mybir.ActivationFunctionType
AX = mybir.AxisListType

LANES = 128
LN_EPS = 1e-5
PI = 3.141592653589793


class Named:
    pass


class Sem:

    def __init__(self, ctx, nc, name):
        self.handle = ctx.enter_context(nc.semaphore(name))
        self.value = 0

    def after(self, instruction, by=1):
        instruction.then_inc(self.handle, by)
        self.value += by
        return self, self.value

    def mark(self):
        return self, self.value


def need(engine, *marks):
    for mark in marks:
        if mark is not None:
            engine.wait_ge(mark[0].handle, mark[1])


def spans(total, step=LANES):
    return [(at, min(step, total - at)) for at in range(0, total, step)]


class Mish:

    def __init__(self, nc, k, sems, x, kept, factor):
        n = x.shape[0]
        self.nc, self.x, self.kept, self.factor = nc, x, kept, factor
        self.half, self.right_angle = k.half[:n, :], k.right_angle[:n, :]
        self.copied, self.angle, self.sine, self.done = sems

    def keep(self, *needed, bias=None):
        v = self.nc.vector
        need(v, *needed)
        self.has_x = self.copied.after(v.tensor_copy(self.kept, self.x) if bias is None else
                                       v.tensor_tensor(self.kept, self.x, bias, ALU.add))
        return self.has_x

    def angles(self, *needed):
        s = self.nc.scalar
        need(s, self.has_x, *needed)
        step = self.angle.after(s.activation(self.factor, self.kept, ACT.Tanh, scale=0.5))
        need(s, step)
        self.has_angle = self.angle.after(s.activation(self.factor, self.factor, ACT.Arctan,
                                                       bias=self.half, scale=-0.5))

    def cosine(self):
        s = self.nc.scalar
        need(s, self.has_angle)
        self.has_factor = self.sine.after(s.activation(self.factor, self.factor, ACT.Sin,
                                                       bias=self.right_angle, scale=-2.0))

    def result(self, out=None, *needed):
        v = self.nc.vector
        need(v, self.has_factor, *needed)
        self.has_result = self.done.after(
            v.tensor_tensor(self.kept if out is None else out, self.kept, self.factor, ALU.mult))
        return self.has_result


def layer_norms(nc, sem, root_sem, xs, outs, stats, moments, eps, needed):
    v, tiles = nc.vector, range(len(xs))
    rows = [slice(0, x.shape[0]) for x in xs]
    marks = list(needed)

    def each(write, semaphore=sem, engine=v):
        for m in tiles:
            need(engine, marks[m])
            marks[m] = semaphore.after(write(m))

    each(lambda m: v.bn_stats(stats[rows[m], m, :], xs[m]))
    each(lambda m: v.bn_aggr(moments[rows[m], m, :], stats[rows[m], m, :]))
    each(lambda m: nc.scalar.activation(moments[rows[m], m, 1:2], moments[rows[m], m, 1:2], ACT.Sqrt,
                                        bias=eps[rows[m], :]), root_sem, nc.scalar)
    each(lambda m: v.reciprocal(moments[rows[m], m, 1:2], moments[rows[m], m, 1:2]))
    each(lambda m: v.tensor_scalar(outs[m], xs[m], moments[rows[m], m, 0:1], moments[rows[m], m, 1:2],
                                   ALU.subtract, ALU.mult))
    return marks


def graph_layer(nc, outer, d, k):
    N, H = d.x.shape
    ED = d.W1c.shape[0]
    KH = H // LANES
    nodes = spans(N)
    NT = len(nodes)
    edges = spans(d.n_edges)
    ET = len(edges)
    pe, act, dve, pool, sp = nc.tensor, nc.scalar, nc.vector, nc.gpsimd, nc.sync

    with ExitStack() as ctx:
        def sb(name, shape, dt=F32):
            return ctx.enter_context(nc.sbuf_tensor(name, shape, dt))

        def sem(name):
            return Sem(ctx, nc, name)

        W1 = sb("W1", [LANES, 2 * KH, H])
        W1c = sb("W1c", [ED, H])
        W2 = sb("W2", [LANES, KH, H])
        W3 = W1
        W4 = sb("W4", [LANES, KH, H])
        b1, b3, b4 = sb("b1", [LANES, H]), sb("b3", [LANES, H]), sb("b4", [LANES, H])
        gamma, beta = sb("gamma", [LANES, H]), sb("beta", [LANES, H])
        b2 = b1
        zeros = sb("zeros", [LANES, H])
        xn = sb("xn", [LANES, NT, H])
        xnT = sb("xnT", [LANES, KH, N])
        stats, moments = sb("stats", [LANES, NT, 6]), sb("moments", [LANES, NT, 2])
        src_ix, dst_ix = sb("src_ix", [LANES, ET], I32), sb("dst_ix", [LANES, ET], I32)
        dst_f = sb("dst_f", [LANES, ET])
        node_no = sb("node_no", [LANES, N])
        proj = [sb(f"proj{n}", [LANES, H]) for n in range(5)]
        GB = 3
        from_src = [sb(f"from_src{n}", [LANES, H]) for n in range(GB)]
        from_dst = [sb(f"from_dst{n}", [LANES, H]) for n in range(GB)]
        EA_TILES = 8
        eaT = [sb(f"eaT{n}", [ED, EA_TILES * LANES]) for n in range(2)]
        onehot = [sb(f"onehot{n}", [LANES, N]) for n in range(2)]
        ROUND, LIVES = 4, 3
        hT = [sb(f"hT{n}", [LANES, KH, LANES]) for n in range(LIVES * ROUND)]
        msg = [sb(f"msg{n}", [LANES, H]) for n in range(LIVES * ROUND)]
        h_factor = [sb(f"h_factor{n}", [LANES, KH, LANES]) for n in range(ROUND)]
        m_factor = [sb(f"m_factor{n}", [LANES, H]) for n in range(ROUND)]
        rows = d.dst_rows.shape[0]
        per_row = d.dst_rows.shape[1] // LANES
        dst_by_tile = sb("dst_by_tile", [rows, per_row * LANES], I32)
        dst_by_tile_f = sb("dst_by_tile_f", [rows, per_row, LANES])
        ends = sb("ends", [rows, per_row, 2])
        ends_chunk = sb("ends_chunk", [rows, per_row, 2])
        ends_i = sb("ends_i", [rows, per_row, 2], I32)
        reach = sb("reach", [1, rows * per_row * 2], I32)
        ps = k.ps
        agg = ps[:NT]
        h_pre = ps[NT]
        m_pre = ps[NT + 1:NT + 3]

        loaded = {n: sem(f"ld_{n}") for n in
                  ("W1", "W1c", "W2", "W3", "W4", "bias", "src", "dst", "dstr", "b2")}
        x_in = [sem(f"x_in{m}") for m in range(NT)]
        q_ready, dve_own = sem("q_ready"), sem("dve_own")

        def load(name, dst, src, engine=sp):
            return loaded[name].after(engine.dma_start(dst, src), 16)

        x_here = []
        for m, (at, n) in enumerate(nodes):
            x_here.append(x_in[m].after(sp.dma_start(k.x1[:n, m, :], d.x[at:at + n, :]), 16))
        W1_here = load("W1", W1[:, :, :], d.W1ab.rearrange("(k p) n -> p k n", p=LANES))
        for t, s in ((b1, d.b1), (b3, d.b3), (b4, d.b4), (gamma, d.gamma), (beta, d.beta)):
            bias_here = load("bias", t[:, :], s.rearrange("(a n) -> a n", a=1).broadcast_to([LANES, H]), act)
        dstr_here = load("dstr", dst_by_tile[:, :], d.dst_rows, act)
        src_here = load("src", src_ix[:, :], d.src_t, act)
        dst_here = load("dst", dst_ix[:, :], d.dst_t, act)
        W1c_here = load("W1c", W1c[:, :], d.W1c)
        W2_here = load("W2", W2[:, :, :], d.W2.rearrange("(k p) n -> p k n", p=LANES))

        consts = sem("gnn_consts")
        consts.after(pool.memset(zeros[:, :], 0.0))
        consts_here = consts.after(pool.iota(node_no[:, :], [[1, N]], base=0, channel_multiplier=0,
                                             allow_small_or_imprecise_dtypes=True))

        root, ln, tr, xnT_ev = sem("root"), sem("ln"), sem("tr"), sem("xnT_ev")
        x_tiles = [k.x1[:n, m, :] for m, (at, n) in enumerate(nodes)]
        y_tiles = [xn[:n, m, :] for m, (at, n) in enumerate(nodes)]
        xn_here = layer_norms(nc, ln, root, x_tiles, y_tiles, stats, moments, k.eps, x_here)
        xnT_here = []
        for m, (at, n) in enumerate(nodes):
            bank = ps[m % 2]
            need(pe, xn_here[m], k.ident_here, xnT_here[m - 2] if m >= 2 else None)
            for c in range(KH):
                last = pe.transpose(bank[:, c * LANES:c * LANES + n], xn[:n, m, c * LANES:(c + 1) * LANES],
                                    k.ident[:n, :n])
            mark = tr.after(last)
            need(act, mark)
            view = bank[:, :].rearrange("p (c n) -> p c n", c=KH)[:, :, :n]
            xnT_here.append(xnT_ev.after(act.activation(xnT[:, :, at:at + n], view, ACT.Copy)))
        pj, pj_ev, pj_out = sem("pj"), sem("pj_ev"), [sem(f"pj_out{n}") for n in range(5)]
        evicted, stored = [None] * 4, [None] * 4
        need(pe, W1_here, *xnT_here[-2:])
        for m, (at, n) in enumerate(nodes):
            for half, dram in enumerate((d.P, d.Q)):
                slot = (2 * m + half) % 4
                bank = ps[2 + slot]
                need(pe, evicted[slot])
                for c in range(KH):
                    last = pe.matmul(bank[:n, :], xnT[:, c, at:at + n], W1[:, half * KH + c, :],
                                     start=(c == 0), stop=(c == KH - 1))
                pj_last = mark = pj.after(last)
                if half == 0:
                    need(act, mark, stored[slot])
                    evicted[slot] = pj_ev.after(act.activation(proj[slot][:n, :], bank[:n, :], ACT.Copy))
                else:
                    need(dve, mark, stored[slot], bias_here)
                    evicted[slot] = q_ready.after(dve.tensor_tensor(proj[slot][:n, :], bank[:n, :], b1[:n, :], ALU.add))
                need(sp, evicted[slot])
                stored[slot] = pj_out[slot].after(sp.dma_start(dram[at:at + n, :], proj[slot][:n, :]), 16)
        need(sp, pj_last, evicted[1], evicted[3])
        load("W3", W3[:, :, :], d.W3.rearrange("(k p) n -> p k n", p=LANES))
        b2_here = load("b2", b2[:, :], d.b2.rearrange("(a n) -> a n", a=1).broadcast_to([LANES, H]))
        load("W4", W4[:, :, :], d.W4.rearrange("(k p) n -> p k n", p=LANES))

        need(dve, dst_here, dstr_here, consts_here)
        step = dve_own.after(dve.tensor_copy(dst_f[:, :], dst_ix[:, :]))
        step = dve_own.after(dve.tensor_copy(dst_by_tile_f[:, :, :],
                                             dst_by_tile[:, :].rearrange("r (a n) -> r a n", n=LANES)))
        need(dve, step)
        dve_own.after(dve.tensor_reduce(ends[:, :, 0], dst_by_tile_f[:, :, :], AX.X, ALU.min))
        step = dve_own.after(dve.tensor_reduce(ends[:, :, 1], dst_by_tile_f[:, :, :], AX.X, ALU.max))
        need(dve, step)
        step = dve_own.after(dve.tensor_scalar(ends_chunk[:, :, :], ends[:, :, :], float(LANES), None, ALU.is_ge))
        for j in range(2, NT):
            need(dve, step)
            step = dve_own.after(dve.scalar_tensor_tensor(ends_chunk[:, :, :], ends[:, :, :], float(j * LANES),
                                                          ends_chunk[:, :, :], ALU.is_ge, ALU.add))
        need(dve, step)
        dst_ready = dve_own.after(dve.tensor_copy(ends_i[:, :, :], ends_chunk[:, :, :]))
        need(sp, dst_ready)
        mark = loaded["dstr"].after(sp.dma_start(d.reach, ends_i[:, :, :].rearrange("r a b -> r (a b)")), 16)
        need(sp, mark)
        reach_here = loaded["dstr"].after(sp.dma_start(reach[:, :], d.reach.rearrange("(o r) c -> o (r c)", o=1)), 16)

        gather_a = [sem(f"gather_a{n}") for n in range(GB)]
        gather_b = [sem(f"gather_b{n}") for n in range(GB)]
        ea_in = [sem(f"ea_in{n}") for n in range(2)]
        h_sem, m_sem, agg_sem = sem("h_sem"), sem("m_sem"), sem("agg_sem")
        h_mish = [sem(f"h_{n}") for n in ("copied", "angle", "sine", "done")]
        m_mish = [sem(f"m_{n}") for n in ("copied", "angle", "sine", "done")]
        hot_sem = sem("hot_sem")
        sum_sem = sem("sum_sem")
        gathered, added, h_done, m_done, agg_done = {}, {}, {}, {}, {}
        h_of, m_of, hot_done, ea_done = {}, {}, {}, {}

        need(pool, *[s for s in stored if s], src_here, dst_here)

        def gather(i):
            at, n = edges[i]
            slot = i % GB
            need(pool, h_done.get(i - GB))
            a = gather_a[slot].after(pool.indirect_dma_start(
                from_src[slot][:n, :], None, d.P, bass.IndirectOffsetOnAxis(ap=src_ix[:n, i:i + 1], axis=0)), 16)
            b = gather_b[slot].after(pool.indirect_dma_start(
                from_dst[slot][:n, :], None, d.Q, bass.IndirectOffsetOnAxis(ap=dst_ix[:n, i:i + 1], axis=0)), 16)
            gathered[i] = (a, b)

        def load_attr(g):
            if g * EA_TILES >= ET:
                return
            at = g * EA_TILES * LANES
            n = min(EA_TILES * LANES, d.n_edges - at)
            need(sp, h_done.get((g - 1) * EA_TILES - 1) if g >= 2 else None)
            ea_done[g] = ea_in[g % 2].after(sp.dma_start(eaT[g % 2][:, :n], d.eaT[:, at:at + n]), 16)

        def add_ends(i):
            n, slot = edges[i][1], i % GB
            need(dve, *gathered[i])
            added[i] = sum_sem.after(dve.tensor_tensor(from_src[slot][:n, :], from_src[slot][:n, :],
                                                       from_dst[slot][:n, :], ALU.add))

        unsignalled = []

        def signalled_by(mark):
            for i in unsignalled:
                agg_done[i] = mark
            unsignalled.clear()

        def first_product(i):
            at, n = edges[i]
            slot, g = i % GB, i // EA_TILES
            need(pe, added[i], ea_done[g], h_of[i - 1].has_x if i else None)
            lo = (i % EA_TILES) * LANES
            for c in range(KH):
                cols = slice(c * LANES, (c + 1) * LANES)
                out = h_pre[:, c * LANES:c * LANES + n]
                pe.matmul(out, from_src[slot][:n, cols], k.ident[:n, :n], start=True, stop=False, is_transpose=True)
                last = pe.matmul(out, W1c[:, cols], eaT[g % 2][:, lo:lo + n], start=False, stop=True)
            h_done[i] = h_sem.after(last)
            signalled_by(h_done[i])

        def second_product(i):
            at, n = edges[i]
            bank = m_pre[i % 2]
            need(pe, h_of[i].has_result, m_of[i - 2].has_x if i >= 2 else None)
            for c in range(KH):
                last = pe.matmul(bank[:n, :], hT[i % len(hT)][:, c, :n], W2[:, c, :],
                                 start=(c == 0), stop=(c == KH - 1))
            m_done[i] = m_sem.after(last)
            signalled_by(m_done[i])

        lowest, highest = pe.alloc_register("lowest_chunk"), pe.alloc_register("highest_chunk")

        def aggregate(i):
            at, n = edges[i]
            pe.reg_load(lowest, reach[0:1, 2 * i:2 * i + 1])
            pe.reg_load(highest, reach[0:1, 2 * i + 1:2 * i + 2])
            need(pe, m_of[i].has_result, hot_done[i])
            for c, (first, width) in enumerate(nodes):
                with pe.If_cmp(lowest, c, "IS_LE"):
                    with pe.If_cmp(highest, c, "IS_GE"):
                        pe.matmul(agg[c][:width, :], onehot[i % 2][:n, first:first + width], msg[i % len(msg)][:n, :],
                                  start=False, stop=True, skip_group_check=True)
                pe.end_ifs()
            unsignalled.append(i)

        for i in range(min(GB, ET)):
            gather(i)
        add_ends(0)
        load_attr(0)
        load_attr(1)
        need(pe, W1c_here, W2_here, consts_here, reach_here, evicted[0], evicted[1], evicted[2], evicted[3])
        for c, (first, width) in enumerate(nodes):
            pe.matmul(agg[c][:width, :], zeros[:, :width], zeros[:, :], start=True, stop=True)

        def keep_h(i):
            n = edges[i][1]
            x = h_pre[:, :].rearrange("p (c n) -> p c n", c=KH)[:, :, :n]
            h_of[i] = Mish(nc, k, h_mish, x, hT[i % len(hT)][:, :, :n], h_factor[i % ROUND][:, :, :n])
            h_of[i].keep(h_done[i], m_done.get(i - len(hT)))

        def keep_m(i):
            n = edges[i][1]
            m_of[i] = Mish(nc, k, m_mish, m_pre[i % 2][:n, :], msg[i % len(msg)][:n, :], m_factor[i % ROUND][:n, :])
            m_of[i].keep(m_done[i], agg_done.get(i - len(msg)), b2_here if i == 0 else None, bias=b2[:n, :])

        def mark_targets(i):
            n = edges[i][1]
            if i - 2 in unsignalled:
                signalled_by(agg_sem.after(pe.drain()))
            need(dve, agg_done.get(i - 2))
            hot_done[i] = hot_sem.after(dve.tensor_scalar(onehot[i % 2][:n, :], node_no[:n, :], dst_f[:n, i:i + 1],
                                                          None, ALU.is_equal))

        def tiles(r):
            return [i for i in range(r * ROUND, (r + 1) * ROUND) if 0 <= i < ET]

        w_in, w_got = [sem(f"w_in{n}") for n in range(2)], sem("w_got")
        w_here, w_done = {}, {}

        def load_weights(q):
            if q < k.w_max.shape[1]:
                need(act, w_done.get(q - 2))
                w_here[q] = w_in[q % 2].after(act.dma_start(
                    k.w_stage[q % 2][:, :], d.W_hh[:, q * k.W_STAGE:(q + 1) * k.W_STAGE]), 16)

        def largest_weight(q):
            need(dve, w_here[q])
            w_done[q] = w_got.after(dve.tensor_reduce(k.w_max[:, q:q + 1], k.w_stage[q % 2][:, :], AX.X, ALU.max,
                                                      apply_absolute_value=True))

        load_weights(0)
        load_weights(1)
        for r in range(-2, -(-ET // ROUND) + 2):
            if 2 <= r < 2 + k.w_max.shape[1]:
                largest_weight(r - 2)
                load_weights(r)
            hs, ms = tiles(r + 1), tiles(r - 1)
            if hs or ms:
                act.preload_act_table_set("sigmoid_and_others")
                for i in hs:
                    h_of[i].angles(h_of[i - ROUND].has_result if i >= ROUND else None)
                for i in ms:
                    m_of[i].angles(m_of[i - ROUND].has_result if i >= ROUND else None)
                for t in [h_of[i] for i in hs] + [m_of[i] for i in ms]:
                    t.cosine()
            for j in range(ROUND):
                a, b, c = (r + 2) * ROUND + j, r * ROUND + j, (r - 2) * ROUND + j
                if 0 <= c < ET:
                    mark_targets(c)
                if a < ET:
                    first_product(a)
                    if a + 1 < ET:
                        add_ends(a + 1)
                    keep_h(a)
                if 0 <= b < ET:
                    second_product(b)
                    keep_m(b)
                if 0 <= c < ET:
                    aggregate(c)
                if j == ROUND - 2:
                    for i in hs:
                        h_of[i].result()
                if j == ROUND - 1:
                    for i in ms:
                        m_of[i].result()
                if a + GB < ET:
                    gather(a + GB)
                if a < ET and a % EA_TILES == EA_TILES - 1:
                    load_attr(a // EA_TILES + 2)

        signalled_by(agg_sem.after(pe.drain()))

        ag_ev, agT, agT_ev, u_sem, u_x, uT, uT_ev, o_sem = (sem(n) for n in (
            "ag_ev", "agT", "agT_ev", "u_sem", "u_x", "uT", "uT_ev", "o_sem"))
        fin, x2T, x2T_ev = sem("fin"), sem("x2T"), sem("x2T_ev")
        u_mish = [sem(f"u_{n}") for n in ("copied", "angle", "sine", "done")]
        W3_here, W4_here = loaded["W3"].mark(), loaded["W4"].mark()
        agg_s = [proj[m] for m in range(NT)]
        aT, uT_s, u_of, u_factor = hT[0:2], hT[2:2 + NT], msg[0:NT], [*m_factor, h_factor[0]]
        u_mi = {}
        marks = {}
        for m, (at, n) in enumerate(nodes):
            need(act, agg_done[ET - 1])
            marks["ag", m] = ag_ev.after(act.activation(agg_s[m][:n, :], agg[m][:n, :], ACT.Copy))
        last_readers = [m_of[ET - 1].has_result, h_of[ET - 1].has_result, m_done[ET - 1]]
        for m, (at, n) in enumerate(nodes):
            need(pe, marks["ag", m], marks.get(("agT_ev", m - 1)), *last_readers)
            for c in range(KH):
                last = pe.transpose(h_pre[:, c * LANES:c * LANES + n], agg_s[m][:n, c * LANES:(c + 1) * LANES],
                                    k.ident[:n, :n])
            marks["agT", m] = agT.after(last)
            need(act, marks["agT", m], marks.get(("u_pre", m - 2)), *last_readers)
            view = h_pre[:, :].rearrange("p (c n) -> p c n", c=KH)[:, :, :n]
            marks["agT_ev", m] = agT_ev.after(act.activation(aT[m % 2][:, :, :n], view, ACT.Copy))
            bank = m_pre[m % 2]
            need(pe, W3_here, marks["agT_ev", m], marks.get(("u_x", m - 2)))
            for c in range(2 * KH):
                lhsT = xnT[:, c, at:at + n] if c < KH else aT[m % 2][:, c - KH, :n]
                last = pe.matmul(bank[:n, :], lhsT, W3[:, c, :], start=(c == 0), stop=(c == 2 * KH - 1))
            marks["u_pre", m] = u_sem.after(last)
            need(dve, marks["u_pre", m])
            marks["u_x", m] = u_x.after(dve.tensor_tensor(u_of[m][:n, :], bank[:n, :], b3[:n, :], ALU.add))
            factor = u_factor[m][:n, :] if m < ROUND else u_factor[m][:n, :, :].rearrange("p c n -> p (c n)")
            u_mi[m] = Mish(nc, k, u_mish, u_of[m][:n, :], u_of[m][:n, :], factor)
            u_mi[m].has_x = marks["u_x", m]
        act.preload_act_table_set("sigmoid_and_others")
        for m in range(NT):
            u_mi[m].angles()
        for m in range(NT):
            u_mi[m].cosine()
        for m in range(NT):
            marks["u", m] = u_mi[m].result()
        for m, (at, n) in enumerate(nodes):
            u = u_of[m][:n, :]
            bank = agg[m]
            need(pe, marks["u", m], marks["ag", m])
            for c in range(KH):
                last = pe.transpose(bank[:, c * LANES:c * LANES + n], u[:, c * LANES:(c + 1) * LANES], k.ident[:n, :n])
            marks["uT", m] = uT.after(last)
            need(act, marks["uT", m])
            view = bank[:, :].rearrange("p (c n) -> p c n", c=KH)[:, :, :n]
            marks["uT_ev", m] = uT_ev.after(act.activation(uT_s[m][:, :, :n], view, ACT.Copy))
        for m, (at, n) in enumerate(nodes):
            bank = agg[m]
            need(pe, W4_here, marks["uT_ev", m])
            for c in range(KH):
                last = pe.matmul(bank[:n, :], uT_s[m][:, c, :n], W4[:, c, :], start=(c == 0), stop=(c == KH - 1))
            marks["o", m] = o_sem.after(last)
            need(dve, marks["o", m])
            marks["y", m] = fin.after(dve.tensor_tensor(y_tiles[m], bank[:n, :], y_tiles[m], ALU.add))

        def each_node_tile(out, in0, in1, op):
            for m, (at, n) in enumerate(nodes):
                need(dve, marks["y", m])
                marks["y", m] = fin.after(dve.tensor_tensor(out(m, n), in0(m, n), in1(m, n), op))

        def y_of(m, n):
            return y_tiles[m]

        each_node_tile(y_of, y_of, lambda m, n: b4[:n, :], ALU.add)
        normed = layer_norms(nc, fin, root, y_tiles, y_tiles, stats, moments, k.eps,
                             [marks["y", m] for m in range(NT)])
        for m in range(NT):
            marks["y", m] = normed[m]
        each_node_tile(y_of, y_of, lambda m, n: gamma[:n, :], ALU.mult)
        each_node_tile(y_of, y_of, lambda m, n: beta[:n, :], ALU.add)
        each_node_tile(lambda m, n: x_tiles[m], lambda m, n: x_tiles[m], y_of, ALU.add)
        xn2_here = layer_norms(nc, fin, root, x_tiles, y_tiles, stats, moments, k.eps,
                               [marks["y", m] for m in range(NT)])
        for m, (at, n) in enumerate(nodes):
            bank = agg[m]
            need(pe, xn2_here[m])
            for c in range(KH):
                last = pe.transpose(bank[:, c * LANES:c * LANES + n], xn[:n, m, c * LANES:(c + 1) * LANES],
                                    k.ident[:n, :n])
            mark = x2T.after(last)
            need(act, mark)
            view = bank[:, :].rearrange("p (c n) -> p c n", c=KH)[:, :, :n]
            marks["x2T_ev", m] = x2T_ev.after(act.activation(k.xn2T[:, :, at:at + n], view, ACT.Copy))
        nc.all_engine_barrier()


GATES = 4
G_IN, G_FORGET, G_INPUT, G_OUT = range(GATES)
H_SCALE = 4096.0
TOP_EXPONENT = 14
PARTS = 3


def power_of_two_scale(nc, k, sem, pe_sem, *needed):
    v, bank = nc.vector, k.ps[7]
    need(v, *needed)
    step = sem.after(v.tensor_reduce(k.w_top[:, 0:1], k.w_max[:, :], AX.X, ALU.max))
    need(nc.tensor, step)
    step = pe_sem.after(nc.tensor.transpose(bank[0:1, 0:LANES], k.w_top[:, 0:1], k.ident[:, :]))
    need(v, step)
    step = sem.after(v.tensor_reduce(k.w_top_row[:, :], bank[0:1, 0:LANES], AX.X, ALU.max))
    need(nc.tensor, step)
    step = pe_sem.after(nc.tensor.matmul(bank[:, LANES:LANES + 1], k.one_row[:, :], k.w_top_row[:, :],
                                         start=True, stop=True))
    need(v, step)
    step = sem.after(v.tensor_copy(k.w_top[:, 0:1], bank[:, LANES:LANES + 1]))
    for write in (
        lambda: v.tensor_scalar(k.exponent[:, :], k.w_top[:, :].bitcast(I32), 23, None, ALU.logical_shift_right),
        lambda: v.tensor_scalar(k.exponent[:, :], k.exponent[:, :], -1, TOP_EXPONENT + 254, ALU.mult, ALU.add),
        lambda: v.tensor_scalar(k.exponent[:, :], k.exponent[:, :], 253, None, ALU.min),
        lambda: v.tensor_scalar(k.w_scale[:, :].bitcast(I32), k.exponent[:, :], 23, None, ALU.logical_shift_left),
        lambda: v.tensor_scalar(k.exponent[:, :], k.exponent[:, :], -1, 254, ALU.mult, ALU.add),
        lambda: v.tensor_scalar(k.w_unscale[:, :].bitcast(I32), k.exponent[:, :], 23, None, ALU.logical_shift_left),
        lambda: v.tensor_scalar(k.w_unscale[:, :], k.w_unscale[:, :], 1.0 / H_SCALE, None, ALU.mult),
    ):
        need(v, step)
        step = sem.after(write())
    return step


def input_products(nc, d, k):
    N, H, S = d.x.shape[0], d.x.shape[1], d.S
    KH = H // LANES
    nodes = spans(N)
    pe, act, dve, pool, sp = nc.tensor, nc.scalar, nc.vector, nc.gpsimd, nc.sync
    with ExitStack() as ctx:
        def sb(name, shape, dt=F32):
            return ctx.enter_context(nc.sbuf_tensor(name, shape, dt))

        def sem(name):
            return Sem(ctx, nc, name)

        WB, OB, PB = 3, 4, 6
        W_in = [sb(f"W_in{n}", [LANES, KH, H]) for n in range(WB)]
        bias_a = [sb(f"bias_a{n}", [LANES, H]) for n in range(2)]
        bias_b = [sb(f"bias_b{n}", [LANES, H]) for n in range(2)]
        parts = [sb(f"parts{n}", [LANES, PARTS, H], BF16) for n in range(OB)]
        sel_x, sel_bias = sb("sel_x", [LANES, KH, S]), sb("sel_bias", [LANES, S])
        logits_out = sb("logits_out", [LANES, len(nodes), S])
        w_stage = k.w_stage
        W_here = [sem(f"W_here{n}") for n in range(WB)]
        bias_here = [sem(f"bias_here{n}") for n in range(2)]
        out_here = [sem(f"xg_out{n}") for n in range(OB)]
        sel_here, xl_out = sem("sel_here"), sem("xl_out")
        stage_here = [sem(f"stage{n}") for n in range(2)]
        bias_sum, xg, hi, lo, xl, xl_ev = (sem(n) for n in ("bias_sum", "xg", "hi", "lo", "xl", "xl_ev"))
        xg_v, xg_a = sem("xg_v"), sem("xg_a")

        sel_here.after(sp.dma_start(sel_x[:, :, :], d.Wsel[:, 2 * KH:3 * KH, :]), 16)
        sel_ready = sel_here.after(sp.dma_start(sel_bias[:, :], d.bsel.rearrange("(a n) -> a n", a=1)
                                                .broadcast_to([LANES, S])), 16)
        weights, biases, summed, products, biased, stored = {}, {}, {}, {}, {}, {}
        first, rest, second, third = {}, {}, {}, {}
        jobs = S * GATES

        def load(j):
            if j >= jobs:
                return
            need(pool, products.get((j - WB, len(nodes) - 1)))
            weights[j] = W_here[j % WB].after(pool.dma_start(W_in[j % WB][:, :, :], d.W_ih[j]), 16)

        def load_bias(j):
            if j >= jobs:
                return
            need(pool, biased.get((j - 2, len(nodes) - 1)))
            for t, s in ((bias_a, d.b_ih), (bias_b, d.b_hh)):
                biases[j] = bias_here[j % 2].after(
                    pool.dma_start(t[j % 2][:, :], s[j:j + 1, :].broadcast_to([LANES, H])), 16)

        for j in range(WB):
            load(j)
        load_bias(0)
        load_bias(1)

        need(pe, sel_ready)
        for m, (at, n) in enumerate(nodes):
            for c in range(KH):
                last = pe.matmul(k.ps[6][:n, m * S:(m + 1) * S], k.xn2T[:, c, at:at + n], sel_x[:, c, :],
                                 start=(c == 0), stop=(c == KH - 1))
        mark = xl.after(last)
        need(dve, mark)
        for m, (at, n) in enumerate(nodes):
            mark = xl_ev.after(dve.tensor_tensor(logits_out[:n, m, :], k.ps[6][:n, m * S:(m + 1) * S],
                                                 sel_bias[:n, :], ALU.add))
            need(sp, mark)
            k.xl_stored = xl_out.after(sp.dma_start(d.XL[at:at + n, :], logits_out[:n, m, :]), 16)

        slices = spans(k.W_hi.shape[1], k.W_STAGE)
        split = {}
        staged = {}

        def stage(q):
            if q >= len(slices):
                return
            at, n = slices[q]
            need(pool, split.get(q - 2))
            staged[q] = stage_here[q % 2].after(pool.dma_start(w_stage[q % 2][:, :n], d.W_hh[:, at:at + n]), 16)

        def split_slice(q):
            at, n = slices[q]
            need(act, staged[q], k.scale_ready)
            high = hi.after(act.activation(k.W_hi[:, at:at + n], w_stage[q % 2][:, :n], ACT.Copy,
                                           scale=k.w_scale[:, :]))
            need(dve, high)
            split[q] = lo.after(dve.scalar_tensor_tensor(k.W_lo[:, at:at + n], w_stage[q % 2][:, :n],
                                                         k.w_scale[:, :], k.W_hi[:, at:at + n],
                                                         ALU.mult, ALU.subtract))
            stage(q + 2)

        order = [(j, m) for j in range(jobs) for m in range(len(nodes))]

        def add_bias(count):
            (j, m), slot = order[count], count % OB
            n, bank = nodes[m][1], k.ps[count % PB]
            need(dve, products[j, m], summed[j])
            biased[j, m] = xg_v.after(dve.tensor_tensor(bank[:n, :], bank[:n, :], bias_a[j % 2][:n, :], ALU.add))
            need(act, biased[j, m], stored.get(count - OB))
            first[count] = xg_a.after(act.copy(parts[slot][:n, 0, :], bank[:n, :]))

        def split_rest(count):
            (j, m), slot = order[count], count % OB
            n, bank = nodes[m][1], k.ps[count % PB]
            need(dve, first[count])
            rest[count] = xg_v.after(dve.tensor_tensor(bank[:n, :], bank[:n, :], parts[slot][:n, 0, :], ALU.subtract))
            need(act, rest[count])
            second[count] = xg_a.after(act.copy(parts[slot][:n, 1, :], bank[:n, :]))

        def store(count):
            (j, m), slot = order[count], count % OB
            (at, n), bank = nodes[m], k.ps[count % PB]
            need(dve, second[count])
            third[count] = xg_v.after(dve.tensor_tensor(parts[slot][:n, 2, :], bank[:n, :], parts[slot][:n, 1, :],
                                                        ALU.subtract))
            need(sp, third[count])
            whole = n // 16 * 16
            for lo_row, rows in ((0, whole), (whole, n - whole)):
                if rows:
                    stored[count] = out_here[slot].after(
                        sp.dma_start(d.XG[at + lo_row:at + lo_row + rows, :, j, :],
                                     parts[slot][lo_row:lo_row + rows, :, :]), 16)

        stage(0)
        stage(1)
        q = 0
        for count in range(len(order) + 2):
            if count < len(order):
                j, m = order[count]
                at, n = nodes[m]
                if m == 0:
                    need(dve, biases[j])
                    summed[j] = bias_sum.after(dve.tensor_tensor(bias_a[j % 2][:, :], bias_a[j % 2][:, :],
                                                                 bias_b[j % 2][:, :], ALU.add))
                need(pe, weights[j] if m == 0 else None, third.get(count - PB))
                for c in range(KH):
                    last = pe.matmul(k.ps[count % PB][:n, :], k.xn2T[:, c, at:at + n], W_in[j % WB][:, c, :],
                                     start=(c == 0), stop=(c == KH - 1))
                products[j, m] = xg.after(last)
                add_bias(count)
            if 0 <= count - 1 < len(order):
                split_rest(count - 1)
            if 0 <= count - 2 < len(order):
                store(count - 2)
            if count < len(order):
                if m % 2 == 1 and q < len(slices):
                    split_slice(q)
                    q += 1
                if m == len(nodes) - 1:
                    load(j + WB)
                    load_bias(j + 2)
        while q < len(slices):
            split_slice(q)
            q += 1
        need(sp, *[stored[len(order) - 1 - n] for n in range(OB)], k.xl_stored)
        nc.all_engine_barrier()


def recurrence(nc, d, k):
    N, H, S = d.x.shape[0], d.x.shape[1], d.S
    KH = H // LANES
    R = PARTS * S * GATES
    pe, act, dve, pool, sp = nc.tensor, nc.scalar, nc.vector, nc.gpsimd, nc.sync
    UNROLL, HALF = 2, 1
    COPIES = ((0, 1), (1, 1), (2, 2))
    assert sum(n for _, n in COPIES) == KH
    AT_UPDATE, AT_H, AT_PICK, AT_COPY = (512,) * 3, (256,), (512,) * 4, (256,)
    ITERATIONS = (N - 1) // UNROLL
    assert 1 + ITERATIONS * UNROLL == N
    with ExitStack() as ctx:
        def sb(name, shape, dt=F32):
            return ctx.enter_context(nc.sbuf_tensor(name, shape, dt))

        def sem(name):
            return Sem(ctx, nc, name)

        cell = [sb(f"cell{n}", [LANES, 5 * KH]) for n in range(2)]
        products = sb("products", [LANES, 2 * KH])
        out_gate, tanh_c = sb("out_gate", [LANES, KH]), sb("tanh_c", [LANES, KH])
        cell_sel = sb("cell_sel", [LANES, KH])
        h = sb("h", [LANES, UNROLL, KH])
        h_pair = sb("h_pair", [LANES, KH, 2], F16)
        gate_rows = sb("gate_rows", [LANES, H])
        x_rows = [sb(f"x_rows{n}", [R, HALF, H], BF16) for n in range(2)]
        x_logits = [sb(f"x_logits{n}", [1, HALF * S]) for n in range(2)]
        x_rows0 = sb("x_rows_first", [R, H], BF16)
        sel_h, sel_c = sb("sel_h", [LANES, KH, S]), sb("sel_c", [LANES, KH, S])
        pick_gate, pick_row = sb("pick_gate", [LANES, GATES]), sb("pick_row", [R, S, GATES], BF16)
        top, which = sb("top", [1, 8]), sb("which", [1, 8], U32)
        history = sb("history", [LANES, N, KH])
        rows_p, gates_p, logits_p = k.ps[0], k.ps[1], k.ps[2]
        gates_by = gates_p[:, 0:GATES * KH].rearrange("p (g c) -> p g c", c=KH)
        XG_rows = d.XG.rearrange("t p r n -> t (p r) n")
        W_hi = k.W_hi[:, :].rearrange("p (s c n) -> p s c n", s=S, c=KH)
        W_lo = k.W_lo[:, :].rearrange("p (s c n) -> p s c n", s=S, c=KH)

        setup, setup_v, first_in = sem("rec_setup"), sem("rec_setup_v"), sem("rec_first")
        x_in = [sem(f"x_in{n}") for n in range(2)]

        def load_half(t, half):
            x_in[half].after(sp.dma_start(x_rows[half][:, :, :],
                                           XG_rows[bass.ds(t, HALF), :, :].rearrange("t r n -> r t n")), 16)
            x_in[half].after(sp.dma_start(x_logits[half][:, :], d.XL1[:, bass.ds(t * S, HALF * S)]), 16)

        first_in.after(sp.dma_start(x_rows0[:, :], XG_rows[0, :, :]), 16)
        first_in.after(sp.dma_start(sel_h[:, :, :], d.Wsel[:, 0:KH, :]), 16)
        first_here = first_in.after(sp.dma_start(sel_c[:, :, :], d.Wsel[:, KH:2 * KH, :]), 16)
        load_half(1, 0)
        load_half(1 + HALF, 1)

        step = setup.after(pool.memset(pick_gate[:, :], 0.0))
        need(pool, step)
        for part in range(2):
            step = setup.after(pool.affine_select(out=pick_gate[:, :], in_=pick_gate[:, :], compare_op=ALU.not_equal,
                                                  fill=1.0, base=-part, pattern=[[-32, GATES]], channel_multiplier=1))
            need(pool, step)
        need(dve, step, first_here, k.scale_ready)
        blocks = k.ident[:R, :R].rearrange("p (a r) -> p a r", a=PARTS)
        row_of = pick_row[:, :, :].rearrange("p s g -> p (s g)")
        need(dve, setup_v.after(dve.tensor_tensor(row_of, blocks[:, 0, :], blocks[:, 1, :], ALU.add)))
        need(dve, setup_v.after(dve.tensor_tensor(row_of, row_of, blocks[:, 2, :], ALU.add)))
        step = setup_v.after(dve.tensor_scalar(pick_gate[:, :], pick_gate[:, :], k.w_unscale[:, :], None, ALU.mult))
        need(dve, step)
        for column in (pick_gate[:, G_IN:G_IN + 1], pick_row[:, :, G_IN:G_IN + 1]):
            setup_v.after(dve.tensor_scalar(column, column, 2.0, None, ALU.mult))
        setup_v.after(dve.tensor_scalar(sel_h[:, :, :], sel_h[:, :, :], 1.0 / H_SCALE, None, ALU.mult))
        setup_v.after(dve.tensor_scalar(sel_c[:, :, :], sel_c[:, :, :], 0.5, None, ALU.mult))
        setup_v.after(dve.memset(rows_p[:, :], 0.0))
        setup_v.after(dve.memset(logits_p[0:1, 0:8], -3.0e38))
        setup_v.after(dve.memset(cell[0][:, :], 0.0))
        step = setup_v.after(dve.memset(cell[1][:, :], 0.0))
        for e in (pe, act, dve, pool):
            need(e, step)
        act.preload_act_table_set("sigmoid_and_others")

        def turn_sem(name, consumer):
            s = sem(name)
            s.consumer = consumer
            return s

        rows_ready, copied = turn_sem("rows_ready", act), turn_sem("copied", pe)
        gates_ready, gates_tanh = turn_sem("gates_ready", act), turn_sem("gates_tanh", dve)
        own, c_act, c_tanh = turn_sem("own", dve), turn_sem("c_act", act), turn_sem("c_tanh", dve)
        picked, logits_ready = turn_sem("picked", pe), turn_sem("logits_ready", dve)
        c_pe, h_ready, pair_ready = (turn_sem(n, pe) for n in ("c_pe", "h_ready", "pair_ready"))
        released = [sem(f"released{n}") for n in range(2)]

        def take_off(*semaphores):
            for s in semaphores:
                s.consumer.sem_inc(s.handle, -s.value)
                s.value = 0

        def keep_clock(widths):
            for columns in widths:
                pe.matmul(k.ps[7][0:2, 0:columns], k.W_hi[:, 0:2], k.W_hi[:, 0:columns], start=True, stop=True)

        def select(u, turn):
            half, v = divmod(u, HALF)
            out, h_before = logits_p[0:1, 0:S], h[:, u, :]
            if v == 0:
                need(pe, (x_in[half], 32))
            pe.matmul(out, k.one_row[0:1, 0:1], x_logits[half][0:1, v * S:(v + 1) * S], start=True, stop=False)
            need(pe, c_pe.mark())
            for c in range(KH):
                pe.matmul(out, cell_sel[:, c:c + 1], sel_c[:, c, :], start=False, stop=False)
            keep_clock(AT_H)
            need(pe, h_ready.mark())
            for c in range(KH):
                last = pe.matmul(out, h_before[:, c:c + 1], sel_h[:, c, :], start=False, stop=(c == KH - 1))
            need(dve, logits_ready.after(last))
            keep_clock(AT_PICK)
            step = own.after(dve.max(top[:, :], logits_p[0:1, 0:8]))
            need(dve, step)
            picked.after(dve.max_index(which[:, :], top[:, :], logits_p[0:1, 0:8]))
            if u == UNROLL - 1:
                dve.tensor_copy(flat[:, bass.ds(turn * (UNROLL * KH), UNROLL * KH)],
                                h[:, :, :].rearrange("p t c -> p (t c)"))
                take_off(own, gates_tanh, c_tanh, logits_ready)

        def x_part(rows, s, stop=False):
            for c in range(KH):
                last = pe.matmul(gates_by[:, :, c], rows[:, c * LANES:(c + 1) * LANES], pick_row[:, s, :],
                                 start=(c == 0), stop=stop, skip_group_check=True)
            return last

        expert = pe.alloc_register("expert")
        flat = history[:, :, :].rearrange("p t c -> p (t c)")

        def gates(u):
            half, v = divmod(u, HALF)
            need(pe, picked.mark())
            pe.reg_load(expert, which[0:1, 0:1])
            need(pe, pair_ready.mark())

            def arm(s):
                for n, part in enumerate((W_hi, W_lo)):
                    for c in range(KH):
                        for g in range(GATES):
                            last = pe.matmul(rows_p[32 * g:32 * g + 2, :], h_pair[:, c, :],
                                             part[:, s, c, g * H:(g + 1) * H], start=(n == c == 0),
                                             stop=(n == 1 and c == KH - 1))
                last.then_inc(rows_ready.handle, 1)
                x_part(x_rows[half][:, v, :], s)

            with pe.If_lt(expert, 2):
                with pe.If_lt(expert, 1):
                    arm(0)
                with pe.Else():
                    arm(1)
            with pe.Else():
                with pe.If_lt(expert, 3):
                    arm(2)
                with pe.Else():
                    arm(3)
            pe.end_ifs()
            if u == UNROLL - 1:
                take_off(rows_ready, gates_ready, c_act, copied, c_pe, h_ready, picked, pair_ready)
                for n in range(2):
                    pe.sem_inc(x_in[n].handle, -32)
            rows_ready.value += 1
            need(act, rows_ready.mark())
            chunk_copied = {}
            for first, count in COPIES:
                at = slice(first * LANES, (first + count) * LANES)
                chunk_copied[first] = copied.after(act.activation(gate_rows[:, at], rows_p[:, at], ACT.Copy))
            keep_clock(AT_COPY)
            for c in range(KH):
                need(pe, chunk_copied.get(c))
                last = pe.matmul(gates_by[:, :, c], gate_rows[:, c * LANES:(c + 1) * LANES], pick_gate[:, :],
                                 start=False, stop=(c == KH - 1), skip_group_check=True)
                if c == 0 and v == HALF - 1:
                    last.then_inc(released[half].handle, 1)
            mark = gates_ready.after(last)
            keep_clock(AT_UPDATE)
            return mark

        def update(u, gates_mark):
            this, following, h_out = cell[u % 2], cell[(u + 1) % 2], h[:, (u + 1) % UNROLL, :]
            need(act, gates_mark)
            tanhs = gates_tanh.after(act.activation(this[:, KH:5 * KH], gates_p[:, 0:GATES * KH], ACT.Tanh, scale=0.5))
            need(dve, tanhs)
            step = own.after(dve.scalar_tensor_tensor(products[:, :], this[:, 2 * KH:4 * KH], 1.0, this[:, 0:2 * KH],
                                                      ALU.add, ALU.mult))
            out_done = own.after(dve.tensor_scalar(out_gate[:, :], this[:, 4 * KH:5 * KH], 1.0, H_SCALE / 2,
                                                   ALU.add, ALU.mult))
            need(dve, step)
            c_done = c_act.after(dve.scalar_tensor_tensor(following[:, 0:KH], products[:, 0:KH], 0.5,
                                                          products[:, KH:2 * KH], ALU.mult, ALU.add))
            c_pe.after(dve.scalar_tensor_tensor(cell_sel[:, :], products[:, 0:KH], 0.5, products[:, KH:2 * KH],
                                                ALU.mult, ALU.add))
            need(act, c_done)
            tc = c_tanh.after(act.activation(tanh_c[:, :], following[:, 0:KH], ACT.Tanh, scale=0.5))
            need(dve, tc, out_done)
            h_ready.after(dve.tensor_tensor(h_out, out_gate[:, :], tanh_c[:, :], ALU.mult))
            step = own.after(dve.tensor_tensor(h_pair[:, :, 0], out_gate[:, :], tanh_c[:, :], ALU.mult))
            need(dve, step)
            pair_ready.after(dve.tensor_tensor(h_pair[:, :, 1], h_out, h_pair[:, :, 0], ALU.subtract))

        need(pe, first_here)
        mark = gates_ready.after(x_part(x_rows0, 0, stop=True))
        update(UNROLL - 1, mark)
        pe.sem_inc(rows_ready.handle, 1)
        act.sem_inc(copied.handle, len(COPIES))
        rows_ready.value, copied.value = 1, len(COPIES)

        engines = bass.OrderedEngineSet([mybir.EngineType.PE, mybir.EngineType.Activation, mybir.EngineType.DVE])
        select(0, None)
        with nc.Fori(0, ITERATIONS, engines=engines) as turn:
            for u in range(UNROLL):
                mark = gates(u)
                update(u, mark)
                select((u + 1) % UNROLL, turn)

        with sp.Fori(0, ITERATIONS - 1) as turn:
            for half in range(2):
                need(sp, (released[half], 1))
                sp.sem_inc(released[half].handle, -1)
                load_half(turn * UNROLL + (1 + UNROLL + half * HALF), half)
        need(sp, (released[0], 1))
        load_half(1, 0)

        hist, back, total, out = sem("hist"), sem("back"), sem("total"), [sem("out_even"), sem("out_odd")]
        need(dve, own.mark())
        hist_here = hist.after(dve.tensor_copy(history[:, N - 1, :], h[:, 0, :]))
        results = [sb(f"result{n}", [LANES, H]) for n in range(2)]
        stored, added = {}, {}
        for m, (at, n) in enumerate(spans(N)):
            bank = k.ps[3 + m % 2]
            need(pe, hist_here, added.get(m - 2))
            for c in range(KH):
                last = pe.transpose(bank[:n, c * LANES:(c + 1) * LANES], history[:, at:at + n, c], k.ident[:, :])
            need(dve, back.after(last), stored.get(m - 2))
            added[m] = total.after(dve.scalar_tensor_tensor(results[m % 2][:n, :], bank[:n, :], 1.0 / H_SCALE,
                                                            k.x1[:n, m, :], ALU.mult, ALU.add))
            need(sp, added[m])
            stored[m] = out[m % 2].after(sp.dma_start(d.out[at:at + n, :], results[m % 2][:n, :]), 16)
        need(sp, stored[m - 1], stored[m])


def program(nc, d):
    with ExitStack() as ctx:
        k = Named()
        H, N = d.x.shape[1], d.x.shape[0]
        KH, S = H // LANES, d.S
        NT = len(spans(N))

        def sb(name, shape, dt=F32):
            return ctx.enter_context(nc.sbuf_tensor(name, shape, dt))

        k.ident = sb("ident", [LANES, LANES])
        k.half, k.right_angle, k.eps = sb("half", [LANES, 1]), sb("right_angle", [LANES, 1]), sb("eps", [LANES, 1])
        k.one_row = sb("one_row", [1, LANES])
        k.x1 = sb("x1", [LANES, NT, H])
        k.xn2T = sb("xn2T", [LANES, KH, N])
        k.W_STAGE = 1024
        k.w_stage = [sb(f"w_stage{n}", [LANES, k.W_STAGE]) for n in range(2)]
        k.w_max = sb("w_max", [LANES, d.W_hh.shape[1] // k.W_STAGE])
        k.w_top, k.w_top_row = sb("w_top", [LANES, 1]), sb("w_top_row", [1, 1])
        k.exponent = sb("exponent", [LANES, 1], I32)
        k.w_scale, k.w_unscale = sb("w_scale", [LANES, 1]), sb("w_unscale", [LANES, 1])
        k.ps = [ctx.enter_context(nc.psum_tensor(f"bank{n}", [LANES, 512], F32)) for n in range(8)]
        ready = Sem(ctx, nc, "ident_ready")
        ready.after(nc.gpsimd.memset(k.ident[:, :], 0.0))
        ready.after(nc.gpsimd.memset(k.half[:, :], 0.5))
        ready.after(nc.gpsimd.memset(k.right_angle[:, :], PI / 2))
        ready.after(nc.gpsimd.memset(k.one_row[:, :], 1.0))
        need(nc.gpsimd, ready.after(nc.gpsimd.memset(k.eps[:, :], LN_EPS)))
        k.ident_here = ready.after(nc.gpsimd.affine_select(
            out=k.ident[:, :], in_=k.ident[:, :], compare_op=ALU.not_equal, fill=1.0, base=0,
            pattern=[[-1, LANES]], channel_multiplier=1))
        need(nc.scalar, k.ident_here)
        graph_layer(nc, ctx, d, k)
        k.W_hi, k.W_lo = (sb(n, [LANES, d.W_hh.shape[1]], F16) for n in ("W_hi", "W_lo"))
        scale_v, scale_pe = Sem(ctx, nc, "scale_v"), Sem(ctx, nc, "scale_pe")
        k.scale_ready = power_of_two_scale(nc, k, scale_v, scale_pe)
        input_products(nc, d, k)
        recurrence(nc, d, k)
def kernel(**inputs):
    import numpy as np
    import concourse.bacc as bacc
    from concourse.bass_utils import run_bass_kernel_spmd as run
    nc = bacc.Bacc("TRN2", target_bir_lowering=False, num_devices=1)
    arrays, d = {}, Named()

    def give(name, a):
        a = np.ascontiguousarray(a)
        arrays["in_" + name] = a
        return nc.dram_tensor("in_" + name, a.shape, mybir.dt.from_np(a.dtype), kind="ExternalInput").ap()

    def by_tile(a):
        tiles = -(-a.shape[0] // LANES)
        full = np.zeros((tiles * LANES,), a.dtype)
        full[:a.shape[0]] = a
        return full.reshape(tiles, LANES)

    H = inputs["x"].shape[1]
    N = inputs["x"].shape[0]
    n_edges = inputs["src"].shape[0]
    W1 = np.asarray(inputs["L0_gnn_W1"])
    d.x = give("x", inputs["x"])
    d.W1ab = give("W1ab", W1[:2 * H])
    d.W1c = give("W1c", W1[2 * H:])
    d.W2, d.W3, d.W4, d.b1, d.b2, d.b3, d.b4, d.gamma, d.beta = (
        give(n, inputs["L0_gnn_" + n]) for n in ("W2", "W3", "W4", "b1", "b2", "b3", "b4", "gamma", "beta"))
    src, dst = np.asarray(inputs["src"]), np.asarray(inputs["dst"])
    d.src_t = give("src_t", by_tile(src).T)
    d.dst_t = give("dst_t", by_tile(dst).T)
    tiles = -(-n_edges // (2 * LANES)) * 2
    rows = np.concatenate([dst, np.repeat(dst[-1:], tiles * LANES - n_edges)])
    d.dst_rows = give("dst_rows", rows.reshape(tiles // 2, 2 * LANES))
    order = [2, 1, 0, 3]
    S = inputs["L0_ffn_W_ih"].shape[0]
    KH = H // LANES
    W_hh = np.asarray(inputs["L0_ffn_W_hh"]).reshape(S, GATES, H, KH, LANES)[:, order]
    d.W_hh = give("W_hh", W_hh.transpose(4, 0, 3, 1, 2).reshape(LANES, -1))
    W_ih = np.asarray(inputs["L0_ffn_W_ih"]).reshape(S, GATES, H, KH, LANES)[:, order]
    d.W_ih = give("W_ih", W_ih.transpose(0, 1, 4, 3, 2).reshape(S * GATES, LANES, KH, H))
    d.b_ih, d.b_hh = (give(n, np.asarray(inputs["L0_ffn_" + n]).reshape(S, GATES, H)[:, order].reshape(S * GATES, H))
                      for n in ("b_ih", "b_hh"))
    d.Wsel = give("Wsel", np.asarray(inputs["L0_ffn_W_sel"]).T.reshape(3 * KH, LANES, S).transpose(1, 0, 2))
    d.bsel = give("bsel", inputs["L0_ffn_b_sel"])
    d.eaT = give("eaT", np.asarray(inputs["edge_attr_64"]).T)
    d.n_edges, d.S = n_edges, S
    d.P = nc.dram_tensor("scratch_P", (N, H), F32, kind="Internal").ap()
    d.Q = nc.dram_tensor("scratch_Q", (N, H), F32, kind="Internal").ap()
    d.reach = nc.dram_tensor("scratch_reach", (tiles // 2, 4), I32, kind="Internal").ap()
    d.XG = nc.dram_tensor("scratch_XG", (N, PARTS, S * GATES, H), BF16, kind="Internal").ap()
    d.XL = nc.dram_tensor("scratch_XL", (N, S), F32, kind="Internal").ap()
    d.XL1 = d.XL.rearrange("(o t) s -> o (t s)", o=1)
    d.out = nc.dram_tensor("out_0", (N, H), F32, kind="ExternalOutput").ap()
    program(nc, d)
    r = run(nc, [arrays], core_ids=[0])
    return r.results[0]["out_0"]
```
